# Optimizing a Trainium2 kernel written in Bass

```python
import numpy as np
import jax
import jax.numpy as jnp

def _softmax(x, axis=-1):
    return jax.nn.softmax(x, axis=axis)
def _gelu(x):
    return jax.nn.gelu(x, approximate=True)
def _silu(x):
    return jax.nn.silu(x)
def _sigmoid(x):
    return jax.nn.sigmoid(x)
def _layernorm(x, axis=-1, eps=1e-5):
    m = jnp.mean(x, axis=axis, keepdims=True)
    v = jnp.var(x, axis=axis, keepdims=True)
    return (x - m) / jnp.sqrt(v + eps)
def _scatter_add(tgt, idx, src, axis=0):
    return tgt.at[idx].add(src)
def _segment_sum(src, seg, n):
    return jax.ops.segment_sum(src, seg, n)

kernel_name = 'mk_adj_preln_d4_adj_128_04a173'

def setup_inputs(seed: int = 0):
    np.random.seed(seed)
    _w = jnp.asarray
    def _rec_inputs():
        import jax
        import jax.numpy as jnp
        _gk = jax.random.key(seed)
        x = -0.000929 + 1 * jax.random.normal(jax.random.fold_in(_gk, 1), (8192, 128), jnp.float32)
        _a = jax.random.bernoulli(jax.random.fold_in(_gk, 2), 0.000976562, (8192, 8192))
        _a = jnp.logical_or(_a, jnp.swapaxes(_a, -1, -2))
        _a = jnp.logical_or(_a, jnp.eye(8192, dtype=bool))
        adj = _a.astype(jnp.int32)
        return x, adj
    x, adj = _rec_inputs()
    def _L0_gnn_setup():
        import jax, jax.numpy as jnp
        import numpy as np
        N = 8192
        D_IN = 128
        D_OUT = 128
        ALPHA = 0.2
        NEG = -9000000000000000.0
        key = jax.random.key(seed)
        k1, k2, k3, k4 = jax.random.split(key, 4)
        input = jax.random.normal(k1, (N, D_IN), dtype=jnp.float32)
        adj = jax.random.randint(k2, (N, N), 0, 2, dtype=jnp.int32)
        lim_w = 1.414 * np.sqrt(6.0 / (D_IN + D_OUT))
        W = jax.random.uniform(k3, (D_IN, D_OUT), jnp.float32, -lim_w, lim_w)
        lim_a = 1.414 * np.sqrt(6.0 / (2 * D_OUT + 1))
        a = jax.random.uniform(k4, (2 * D_OUT, 1), jnp.float32, -lim_a, lim_a)
        return {'input': input, 'adj': adj, 'W': W, 'a': a}
    _L0_gnn_all = _L0_gnn_setup()
    _L0_gnn_in = {k: v for k, v in _L0_gnn_all.items() if k in ('W', 'a', )}
    del _L0_gnn_all

    def _L1_gnn_setup():
        import jax, jax.numpy as jnp
        import numpy as np
        N = 8192
        IN = 128
        OUT = 128
        THR = 0.0001
        ALPHA = 0.2
        NEG = -1000000000.0
        key = jax.random.key(seed)
        k1, k2, k3, k4 = jax.random.split(key, 4)
        inp = jax.random.normal(k1, (N, IN), jnp.float32)
        W = jax.random.normal(k2, (IN, OUT), jnp.float32) * (1.414 * np.sqrt(2.0 / (IN + OUT)))
        a = jax.random.normal(k3, (2 * OUT, 1), jnp.float32) * (1.414 * np.sqrt(2.0 / (2 * OUT + 1)))
        adj = jax.random.randint(k4, (N, N), 0, 2, jnp.int32)
        return {'input': inp, 'W': W, 'a': a, 'adj': adj, 'M': N}
    _L1_gnn_all = _L1_gnn_setup()
    _L1_gnn_in = {k: v for k, v in _L1_gnn_all.items() if k in ('W', 'a', )}
    del _L1_gnn_all

    def _L2_gnn_setup():
        import jax, jax.numpy as jnp
        import numpy as np
        N, D = (8192, 128)
        key = jax.random.key(seed)
        k1, k2, k3 = jax.random.split(key, 3)
        adj = jax.random.randint(k1, (N, N), 0, 2, dtype=jnp.int32)
        emb = jax.random.normal(k2, (N, D), dtype=jnp.float32)
        attn = jax.random.normal(k3, (2 * D, 1), dtype=jnp.float32)
        return {'adj': adj, 'emb': emb, 'attn': attn}
    _L2_gnn_all = _L2_gnn_setup()
    _L2_gnn_in = {k: v for k, v in _L2_gnn_all.items() if k in ('attn', )}
    del _L2_gnn_all

    def _L3_gnn_setup():
        import jax
        import jax.numpy as jnp
        import numpy as np
        from jax import lax
        N = 8192
        F = 128
        CHUNK = 64
        key = jax.random.key(seed)
        kx, ka = jax.random.split(key)
        X = jax.random.normal(kx, (N, F), dtype=jnp.float32)
        adj = jax.random.randint(ka, (N, N), 0, 2, dtype=jnp.int32)
        return {'X': X, 'adj': adj}
    _L3_gnn_all = _L3_gnn_setup()
    _L3_gnn_in = {k: v for k, v in _L3_gnn_all.items() if k in ()}
    del _L3_gnn_all

    return {
        "x": x,
        "adj": adj,
        "L0_gnn_W": _L0_gnn_in["W"],
        "L0_gnn_a": _L0_gnn_in["a"],
        "L1_gnn_W": _L1_gnn_in["W"],
        "L1_gnn_a": _L1_gnn_in["a"],
        "L2_gnn_attn": _L2_gnn_in["attn"],
    }

def reference(x, adj, L0_gnn_W, L0_gnn_a, L1_gnn_W, L1_gnn_a, L2_gnn_attn):
    import jax
    import jax.numpy as jnp
    def _L0_gnn_ref(input, adj, W, a):
        import jax, jax.numpy as jnp
        import numpy as np
        N = 8192
        D_IN = 128
        D_OUT = 128
        ALPHA = 0.2
        NEG = -9000000000000000.0
        h = input @ W
        a1 = a[:D_OUT, 0]
        a2 = a[D_OUT:, 0]
        e = (h @ a1)[:, None] + (h @ a2)[None, :]
        e = jnp.where(e > 0, e, ALPHA * e)
        e = jnp.where(adj > 0, e, NEG)
        attention = jax.nn.softmax(e, axis=1)
        h_prime = attention @ h
        return jax.nn.elu(h_prime)

    def _L1_gnn_ref(input, W, a, adj, M):
        import jax, jax.numpy as jnp
        import numpy as np
        N = 8192
        IN = 128
        OUT = 128
        THR = 0.0001
        ALPHA = 0.2
        NEG = -1000000000.0
        h = input @ W
        a_src = a[:OUT, 0]
        a_dst = a[OUT:, 0]
        e = jax.nn.leaky_relu((h[:M] @ a_src)[:, None] + (h @ a_dst)[None, :], negative_slope=ALPHA)
        valid = (adj[:M] > 0) & (h.sum(axis=1) != 0)[None, :]
        att = jax.nn.softmax(jnp.where(valid, e, NEG), axis=1)
        att = jnp.where(valid, att, 0.0)
        L = valid.sum(axis=1).astype(h.dtype)
        top = att.max(axis=1)
        attention = jnp.where(att >= THR, att, 0.0) * L[:, None]
        attention = jnp.where((top > THR)[:, None], attention, 0.0)
        h_prime = attention @ h
        return jax.nn.elu(h[:M] + h_prime)

    def _L2_gnn_ref(adj, emb, attn):
        import jax, jax.numpy as jnp
        import numpy as np
        N, D = (8192, 128)
        d = emb.shape[1]
        s_i = emb @ attn[:d]
        s_j = emb @ attn[d:]
        e = jax.nn.leaky_relu(s_i + s_j.T, negative_slope=0.2)
        neg_inf = jnp.float32(-1000000000.0)
        e = e + jnp.where(adj > 0, jnp.float32(0.0), neg_inf)
        alpha = jax.nn.softmax(e, axis=1)
        return alpha @ emb

    def _L3_gnn_ref(X, adj):
        import jax
        import jax.numpy as jnp
        import numpy as np
        from jax import lax
        N = 8192
        F = 128
        CHUNK = 64
        neg = jnp.finfo(X.dtype).min
        mask = adj != 0
        n, f = X.shape

        def body(_, mrows):
            vals = jnp.max(jnp.where(mrows[:, :, None], X[None, :, :], neg), axis=1)
            has_nbr = jnp.any(mrows, axis=1)
            return (None, jnp.where(has_nbr[:, None], vals, jnp.zeros((), X.dtype)))
        _, out = lax.scan(body, None, mask.reshape(n // CHUNK, CHUNK, n))
        return out.reshape(n, f)

    h = jnp.maximum(_layernorm(x, axis=-1), 0.0)
    x = x + _L0_gnn_ref(h, adj, L0_gnn_W, L0_gnn_a)
    h = jnp.maximum(_layernorm(x, axis=-1), 0.0)
    x = x + _L1_gnn_ref(h, L1_gnn_W, L1_gnn_a, adj, 8192)
    h = jnp.maximum(_layernorm(x, axis=-1), 0.0)
    x = x + _L2_gnn_ref(adj, h, L2_gnn_attn)
    h = jnp.maximum(_layernorm(x, axis=-1), 0.0)
    x = x + _L3_gnn_ref(h, adj)
    return x


_drawn_inputs = setup_inputs


def setup_inputs(seed=0):
    import zlib

    import numpy as np

    out = dict(_drawn_inputs(seed))
    spreads = {}
    factors = {}
    for name, (base, spread) in spreads.items():
        noise = np.random.default_rng([zlib.crc32(name.encode()), seed]).standard_normal(out[name].shape)
        drawn = base * np.exp(spread * noise) if base else spread * noise
        out[name] = jnp.asarray(drawn.astype(out[name].dtype))
    for name, factor in factors.items():
        out[name] = (out[name] * factor).astype(out[name].dtype)
    return out
```

```python
from contextlib import ExitStack

import concourse.bass as bass
from concourse import mybir

ALU = mybir.AluOpType
ACT = mybir.ActivationFunctionType
F32 = mybir.dt.float32
BF16 = mybir.dt.bfloat16
I32 = mybir.dt.int32
U32 = mybir.dt.uint32
AX_X = mybir.AxisListType.X

P = 128
BLK = 256
TOP = 8
KMAX = 40
DMAX = KMAX - 1
EPS = 1e-5
SLOPE = 0.2
THR = 1e-4
NEG0 = 9000000000000000.0
NEG1 = 1000000000.0
FAR = -1e30
LAYERS = 4
EDGE_P = 1.0 - (1.0 - 0.000976562) ** 2

R_TAB, R_OUT, R_S, R_X = KMAX, KMAX + 1, KMAX + 2, KMAX + 4


def tile_capacities(n):
    pm = (1.0 - EDGE_P) ** (n - 1)
    at_most = []
    for k in range(1, KMAX + 1):
        at_most.append((at_most[-1] if at_most else 0.0) + pm)
        pm *= (n - k) / k * EDGE_P / (1.0 - EDGE_P)
    caps = []
    for first in range(0, n, 2 * P):
        cap = DMAX
        if first:
            for d in range(DMAX, 0, -1):
                above = max(n * (1.0 - at_most[d]), 0.0)
                if above + 4.0 * above ** 0.5 <= first:
                    cap = d
        caps.append(cap)
    return caps


def build(nc, x, adj, w0, a0, w1, a1, a2, out):
    N, F = x.shape
    T = N // P
    PAIRS = T // 2
    NBLK = N // BLK
    CAND = NBLK * TOP
    POOL_BLK = NBLK * 7 // 8
    RW = R_X + F
    TW = F + 4
    XW = F + TW
    X_T, X_S = 2 * F, 2 * F + 1
    CAPS = tile_capacities(N)
    assert F == P and CAPS[0] == DMAX and N % BLK == 0

    groups = []
    for i, c in enumerate(CAPS):
        if i > 1 and groups[-1][2] == c:
            groups[-1][1] = i + 1
        else:
            groups.append([i, i + 1, c])
    slots_before = [0]
    for c in CAPS:
        slots_before.append(slots_before[-1] + c)
    LAYER_SLOTS = slots_before[-1]

    def gathers(l, first, i, cap):
        n = slots_before[first] + (i - first) * cap
        return (n + i if l == 0 else n + LAYER_SLOTS * l + PAIRS)

    srt = nc.dram_tensor("sorted_records", [N, RW], F32).ap()
    kept = [None] + [nc.dram_tensor(f"kept{l}", [N, XW], F32).ap() for l in (1, 2, 3)]
    table = [nc.dram_tensor(f"table{l}", [N + 1, TW], F32).ap() for l in range(LAYERS)]

    with ExitStack() as ctx:
        def sb(name, shape, dt=F32):
            return ctx.enter_context(nc.sbuf_tensor(name, shape, dt))

        def sem(name):
            return ctx.enter_context(nc.semaphore(name))

        def sems(name):
            return [sem(f"{name}{b}") for b in range(2)]

        NG = KMAX * TW
        C = KMAX
        CT = C * T
        arena = sb("arena", [P, max(2 * N, 2 * NG, 4 * CT)])
        adj_t = arena[:, 0:2 * N].bitcast(I32).rearrange("p (b n) -> p b n", b=2)
        gath = [arena[:, b * NG:(b + 1) * NG].rearrange("p (k w) -> p k w", w=TW) for b in range(2)]
        totals, scan, value, ones_ct = (arena[:, i * CT:(i + 1) * CT] for i in range(4))
        sq_all = sb("sq_all", [P, 2 * N], BF16)
        sq = [sq_all[:, b * N:(b + 1) * N] for b in range(2)]
        rec = sb("rec", [P, T, RW])
        eq = sb("eq", [P, CT], BF16)
        deg = sb("deg", [P, T])
        squares = sb("squares", [P, T])
        rank = sb("rank", [P, T])
        rank_u = sb("rank_u", [P, T], U32)
        flags = sb("flags", [P, T])
        bad = sb("bad", [P, 4])
        bad_sum = sb("bad_sum", [P, 1])
        verdict = sb("verdict", [P, 1], I32)
        pos = sb("pos", [P, BLK], BF16)
        blk_base = sb("blk_base", [P, NBLK, TOP])
        cls = sb("cls", [P, C])
        limit = sb("limit", [P, C])
        tri = sb("tri", [P, P], BF16)
        ones_b = sb("ones_b", [P, P], BF16)
        ones_f = sb("ones_f", [P, P])
        ident = sb("ident", [P, P])
        node = sb("node", [P, T, 2], U32)
        node_f = sb("node_f", [P, T])
        eps = sb("eps", [P, 1])
        w_sb = [sb(f"w{l}_sb", [P, F]) for l in range(2)]
        wT = [sb(f"wT{l}", [P, F]) for l in range(2)]
        att = [sb(f"att{l}", [P, 2]) for l in range(3)]
        wx = [sb(f"wx{l}", [P, F + 2]) for l in range(2)]
        no_row = sb("no_row", [1, TW])
        cand = sb("cand", [P, 2, NBLK, TOP], BF16)
        cand_b = sb("cand_b", [P, 2, NBLK, TOP])
        cand_g = sb("cand_g", [P, 2, CAND])
        lst = sb("lst", [P, 2, KMAX])
        lst_c = sb("lst_c", [P, 2, KMAX])
        stats = sb("stats", [P, 6])
        mv = sb("mv", [P, 2, 2])
        std = sb("std", [P, 2])
        rstd = sb("rstd", [P, 1])
        xn = sb("xn", [P, 2, F])
        hn = sb("hn", [P, 2, F])
        hnT = sb("hnT", [P, 2, F])
        new = sb("new", [P, 2, XW])
        hsum = sb("hsum", [P, 2])
        hzero = sb("hzero", [P, 1])
        idx = [sb(f"idx{b}", [P, R_S], U32) for b in range(2)]
        row = sb("row", [P, 2, XW])
        rid = [sb(f"rid{b}", [P, 2], U32) for b in range(2)]
        e1 = sb("e1", [P, KMAX])
        e2 = sb("e2", [P, 2, KMAX])
        emax = sb("emax", [P, 1])
        nemax = sb("nemax", [P, 2])
        prob = sb("prob", [P, 2, KMAX])
        psum_p = sb("psum_p", [P, 2])
        ok = sb("ok", [P, KMAX])
        count = sb("count", [P, 1])
        pok = sb("pok", [P, KMAX])
        sums = sb("sums", [P, 1])
        rsum = sb("rsum", [P, 1])
        share = sb("share", [P, KMAX])
        top = sb("top", [P, 1])
        wgt = sb("wgt", [P, KMAX])
        fac = sb("fac", [P, 1])
        agg = sb("agg", [P, F])
        z = sb("z", [P, 2, F])
        zneg = sb("zneg", [P, 2, F])
        ez = sb("ez", [P, 2, F])
        z1 = sb("z1", [P, F])

        banks = ctx.enter_context(nc.psum_tensor("banks", [P, 8, 512], F32))
        hT_ps, hw_ps = banks[:, 0:2, :], banks[:, 2:4, :]
        rank_ps = banks[:, 3:8, :].rearrange("p b n -> p (b n)")
        assert CT <= 5 * 512
        CT_CHUNKS = [(c, min(c + 512, CT)) for c in range(0, CT, 512)]

        d_adj, d_neg, d_score = adj_t[:, 0, :], arena[:, 0:N], arena[:, N:2 * N]
        d_mask = rec[:, :, :].rearrange("p t w -> p (t w)").bitcast(BF16)[:, 0:N]
        d_t = sq_all[:, :].bitcast(F32)
        d_tcol, d_h, d_part = flags, ez[:, 1, :], z[:, 1, :]
        t_all = [nc.dram_tensor(f"t_all{l}", [T, P], F32).ap() for l in range(3)]

        const_pool, const_dve = sem("const_pool"), sem("const_dve")
        w_in, dummy_set, dummy_out = sem("w_in"), sem("dummy_set"), sem("dummy_out")
        wT_ps, wT_sb, wa_ps, wx_done = sem("wT_ps"), sem("wT_sb"), sem("wa_ps"), sem("wx_done")
        adj_in, x_in = sems("adj_in"), sems("x_in")
        recx_in = sem("recx_in")
        sq_done, key_pool, key_dve = sem("sq_done"), sem("key_pool"), sem("key_dve")
        max_done, cb_done, cg_done = sem("max_done"), sem("cb_done"), sem("cg_done")
        round_done, lst_free = sems("round_done"), sem("lst_free")
        self_out = sem("self_out")
        own_done = sem("own_done")
        deg_done, passed = sem("deg_done"), sem("passed")
        st_done, mv_done, std_done, rstd_done = sem("st_done"), sem("mv_done"), sem("std_done"), sem("rstd_done")
        xn_done, hn_done, hT_done, hnT_done = sem("xn_done"), sem("hn_done"), sem("hT_done"), sem("hnT_done")
        hw_done, row_done = sem("hw_done"), sem("row_done")
        hzero_done, tflag_done = sem("hzero_done"), sem("tflag_done")
        s_kept = sem("s_kept")
        tab_nat = sems("tab_nat")
        dv, tot_ps, tot_sb, tri_ps, bad_ps, verdict_done = (
            sem("dv"), sem("tot_ps"), sem("tot_sb"), sem("tri_ps"), sem("bad_ps"), sem("verdict_done"))
        sorted_out = sem("sorted_out")
        idx_in, row_in, g_in = sems("idx_in"), sems("row_in"), sems("g_in")
        rid_done, x_new = sem("rid_done"), sem("x_new")
        e1_done, e2_done, emax_done, nemax_done, prob_done = (
            sem("e1_done"), sem("e2_done"), sem("emax_done"), sem("nemax_done"), sem("prob_done"))
        ok_done, pok_done, sums_done, share_done, top_done, wgt_done = (
            sem("ok_done"), sem("pok_done"), sem("sums_done"), sem("share_done"), sem("top_done"), sem("wgt_done"))
        rsum_done, fac_done, gw_done, agg_done, z_done, zneg_done, ez_done, z1_done = (
            sem("rsum_done"), sem("fac_done"), sem("gw_done"), sem("agg_done"), sem("z_done"),
            sem("zneg_done"), sem("ez_done"), sem("z1_done"))
        d_in, d_t_in, d_h_in, d_row_in = sem("d_in"), sem("d_t_in"), sem("d_h_in"), sem("d_row_in")
        d_mask_done, d_ok_done, d_neg_done, d_add_done = sem("d_mask_done"), sem("d_ok_done"), sem("d_neg_done"), sem("d_add_done")
        d_cnt_done, d_clear_done = sem("d_cnt_done"), sem("d_clear_done")
        d_part_done, d_partT_done, d_turn_done, d_mm_done, d_acc_done = (
            sem("d_part_done"), sem("d_partT_done"), sem("d_turn_done"), sem("d_mm_done"), sem("d_acc_done"))
        d_rmask_done, d_prod_done, d_max_done, d_col_done = (
            sem("d_rmask_done"), sem("d_prod_done"), sem("d_max_done"), sem("d_col_done"))
        d_kept_out, d_tab_out, d_out = sem("d_kept_out"), sem("d_tab_out"), sem("d_out")
        kept_out, tab_out, res_out = sems("kept_out"), sems("tab_out"), sems("res_out")

        block = ctx.enter_context(nc.Block())

        def at_least(eng, s, v):
            if not isinstance(v, int) or v > 0:
                eng.wait_ge(s, v)

        def pairs_of(eng, first, last):
            if last - first == 1:
                yield first
            else:
                with eng.Fori(first, last) as i:
                    yield i

        def rows_of(dram, tile, first=0):
            if isinstance(tile, int):
                return dram[tile * P + first:tile * P + first + P, :]
            return dram[bass.ds(tile * P + first, P), :]

        def node_dve_stats(dve, b, m, xin):
            nc.vector.bn_stats(stats[:], xin).then_inc(st_done, 1)
            dve.wait_ge(st_done, m + 1)
            dve.sem_inc(passed, 1)
            nc.vector.bn_aggr(mv[:, b, :], stats[:]).then_inc(mv_done, 1)

        def node_dve_norm(dve, b, m, xin):
            dve.wait_ge(std_done, m + 1)
            nc.vector.reciprocal(rstd[:], std[:, b:b + 1]).then_inc(rstd_done, 1)
            dve.wait_ge(rstd_done, m + 1)
            nc.vector.tensor_scalar(xn[:, b, :], xin, mv[:, b, 0:1], rstd[:], ALU.subtract, ALU.mult).then_inc(xn_done, 1)

        def node_act_std(act, b, m):
            act.wait_ge(mv_done, m + 1)
            nc.scalar.activation(std[:, b:b + 1], mv[:, b, 1:2], ACT.Sqrt, bias=eps[:]).then_inc(std_done, 1)

        def node_act(act, b, m, layer, scattered):
            h_row = new[:, b, F:2 * F]
            scattered()
            act.wait_ge(xn_done, m + 1)
            nc.scalar.activation(h_row if layer > 1 else hn[:, b, :], xn[:, b, :], ACT.Relu).then_inc(hn_done, 1)
            if layer == 3:
                return
            act.wait_ge(hT_done, m + 1)
            nc.scalar.activation(hnT[:, b, :], hT_ps[:, b, 0:P], ACT.Copy).then_inc(hnT_done, 1)
            act.wait_ge(hw_done, m + 1)
            if layer == 2:
                nc.scalar.activation(new[:, b, X_T:X_T + 2], hw_ps[:, b, 0:2], ACT.Copy).then_inc(row_done, 1)
            else:
                nc.scalar.activation(h_row, hw_ps[:, b, 0:F], ACT.Copy, accum_out=hsum[:, b:b + 1]).then_inc(row_done, 1)
                nc.scalar.activation(new[:, b, X_T:X_T + 2], hw_ps[:, b, F:F + 2], ACT.Copy).then_inc(row_done, 1)

        def node_pe(pe, b, m, layer):
            if layer == 3:
                return
            h_in = new[:, b, F:2 * F] if layer == 2 else hn[:, b, :]
            pe.wait_ge(hn_done, m + 1)
            nc.tensor.transpose(hT_ps[:, b, 0:P], h_in, ident[:]).then_inc(hT_done, 1)
            pe.wait_ge(hnT_done, m + 1)
            if layer == 2:
                nc.tensor.matmul(hw_ps[:, b, 0:2], hnT[:, b, :], att[2][:], start=True, stop=True).then_inc(hw_done, 1)
            else:
                nc.tensor.matmul(hw_ps[:, b, 0:F + 2], hnT[:, b, :], wx[layer][:], start=True, stop=True).then_inc(hw_done, 1)

        def rows_in(l, i):
            return 32 * (i + 1) if l == 0 else 16 * (PAIRS * (l + 1) + i + 1)

        def rows_after(layer, t):
            return [2 * (t + 1), 2 * T + 2 * (t + 1), 4 * T + t + 1][layer]

        def row_sources(l, t):
            x_from = rows_of(x, t) if l == 0 else rows_of(kept[l][:, 0:F], t)
            return x_from, rows_of(table[l], t, 1)

        def dense_loads(sp):
            for l in range(3):
                if l:
                    sp.wait_ge(d_kept_out, 16 * T * l)
                    sp.wait_ge(d_tab_out, 16 * T * l)
                else:
                    for b in range(2):
                        sp.wait_ge(tab_nat[b], 16 * PAIRS)
                sp.dma_start(d_tcol[:, 0:T], table[l][1:N + 1, F:F + 1].rearrange("(t p) w -> p (t w)", p=P),
                             allow_slow_non_contiguous=True).then_inc(d_t_in, 16)
                sp.wait_ge(d_t_in, 48 * l + 16)
                sp.dma_start(t_all[l].rearrange("t p -> p t"), d_tcol[:, 0:T],
                             allow_slow_non_contiguous=True).then_inc(d_t_in, 16)
                sp.wait_ge(d_t_in, 48 * l + 32)
                sp.dma_start(d_t, t_all[l].rearrange("t p -> (t p)")[None, :].broadcast_to([P, N])).then_inc(d_t_in, 16)
                with sp.Fori(0, T) as t:
                    x_from, h_from = row_sources(l, t)
                    sp.dma_start(d_adj, rows_of(adj, t)).then_inc(d_in, 16)
                    sp.dma_start(row[:, 0, 0:F], x_from).then_inc(d_in, 16)
                    sp.dma_start(row[:, 0, F:XW], h_from).then_inc(d_in, 16)
                    with sp.Fori(0, T) as c:
                        sp.dma_start(d_h, rows_of(table[l][:, 0:F], c, 1)).then_inc(d_h_in, 16)
                        sp.wait_ge(d_mm_done, (T * l + t) * T + c + 1)
                        sp.sem_inc(passed, 1)
                    sp.wait_ge(mv_done, T * (l + 1) + t + 1)
                    sp.sem_inc(passed, 1)
            sp.wait_ge(d_kept_out, 16 * T * 3)
            sp.wait_ge(d_tab_out, 16 * T * 3)
            with sp.Fori(0, T) as c:
                sp.dma_start(d_h, rows_of(table[3][:, 0:F], c, 1)).then_inc(d_h_in, 16)
                sp.wait_ge(d_partT_done, 3 * T * T + c + 1)
                sp.sem_inc(passed, 1)
            with sp.Fori(0, N) as i:
                sp.dma_start(d_adj, adj[bass.ds(i, 1), :].broadcast_to([P, N])).then_inc(d_row_in, 16)
                sp.wait_ge(d_col_done, i + 1)
                sp.sem_inc(passed, 1)
            with sp.Fori(0, T) as t:
                sp.dma_start(row[:, 0, 0:F], rows_of(kept[3][:, 0:F], t)).then_inc(d_in, 16)
                sp.wait_ge(x_new, 3 * T + t + 1)
                sp.sem_inc(passed, 1)
                sp.dma_start(rows_of(out, t), new[:, 0, 0:F]).then_inc(d_out, 16)
                sp.wait_ge(d_out, 16 * (t + 1))
                sp.sem_inc(passed, 1)

        def dense_pe(pe):
            for l in range(3):
                with pe.Fori(0, T) as t:
                    with pe.Fori(0, T) as c:
                        q = (T * l + t) * T + c
                        pe.wait_ge(d_part_done, q + 1)
                        nc.tensor.transpose(hT_ps[:, 0, 0:P], d_part, ident[:]).then_inc(d_partT_done, 1)
                        pe.wait_ge(d_turn_done, q + 1)
                        pe.wait_ge(d_h_in, 16 * (q + 1))
                        nc.tensor.matmul(hw_ps[:, 0, 0:F], hnT[:, 0, :], d_h, start=True, stop=True).then_inc(d_mm_done, 1)
                    node_pe(pe, 0, T * (l + 1) + t, l + 1)
            with pe.Fori(0, T) as c:
                pe.wait_ge(d_h_in, 16 * (3 * T * T + c + 1))
                pe.wait_ge(hn_done, 4 * T)
                nc.tensor.transpose(hT_ps[:, 0, 0:P], d_h, ident[:]).then_inc(d_partT_done, 1)
                pe.wait_ge(d_turn_done, 3 * T * T + c + 1)
                pe.sem_inc(passed, 1)
            with pe.Fori(0, T) as t:
                pe.wait_ge(d_part_done, 3 * T * T + t + 1)
                nc.tensor.transpose(hT_ps[:, 0, 0:P], d_part, ident[:]).then_inc(d_partT_done, 1)

        def dense_act(act):
            act.wait_ge(dummy_out, 16 * LAYERS)
            act.wait_ge(recx_in, 16 * T)
            for l in range(3):
                with act.Fori(0, T) as t:
                    g = T * l + t
                    m = T + g
                    act.wait_ge(nemax_done, g + 1)
                    nc.scalar.activation(d_score, d_score, ACT.Exp, bias=nemax[:, 0:1],
                                         accum_out=psum_p[:, 0:1]).then_inc(prob_done, 1)
                    with act.Fori(0, T) as c:
                        act.wait_ge(d_partT_done, g * T + c + 1)
                        nc.scalar.activation(hnT[:, 0, :], hT_ps[:, 0, 0:P], ACT.Copy).then_inc(d_turn_done, 1)
                    if l < 2:
                        act.wait_ge(zneg_done, g + 1)
                        nc.scalar.activation(ez[:, 0, :], zneg[:, 0, :], ACT.Exp).then_inc(ez_done, 1)
                    node_act_std(act, 0, m)
                    node_act(act, 0, m, l + 1, lambda: None)
                    if l == 0:
                        act.wait_ge(tflag_done, t + 1)
                    if l == 1:
                        act.wait_ge(row_done, rows_after(2, t))
                    if l == 2:
                        act.wait_ge(hn_done, m + 1)
                    act.dma_start(rows_of(kept[l + 1], t), new[:, 0, :]).then_inc(d_kept_out, 16)
                    act.dma_start(rows_of(table[l + 1], t, 1), new[:, 0, F:XW]).then_inc(d_tab_out, 16)
                    act.wait_ge(d_kept_out, 16 * (g + 1))
                    act.wait_ge(d_tab_out, 16 * (g + 1))
                    act.sem_inc(passed, 1)
            with act.Fori(0, T) as c:
                act.wait_ge(d_partT_done, 3 * T * T + c + 1)
                act.sem_inc(passed, 1)
                nc.scalar.activation(d_score[:, bass.ds(c * P, P)], hT_ps[:, 0, 0:P], ACT.Copy).then_inc(d_turn_done, 1)

        def dense_dve(dve):
            for l in range(3):
                dve.wait_ge(d_t_in, 48 * (l + 1))
                with dve.Fori(0, T) as t:
                    g = T * l + t
                    m = T + g
                    big = (NEG0, NEG1, NEG1)[l]
                    dve.wait_ge(d_in, 48 * (g + 1))
                    nc.vector.tensor_scalar(d_mask, d_adj, 0.0, None, ALU.is_gt).then_inc(d_mask_done, 1)
                    dve.wait_ge(d_mask_done, g + 1)
                    if l == 1:
                        nc.vector.tensor_scalar(d_score, d_t, FAR / 10, None, ALU.is_gt).then_inc(ok_done, 1)
                        dve.wait_ge(ok_done, t + 1)
                        nc.vector.tensor_tensor(d_mask, d_mask, d_score, ALU.mult).then_inc(d_ok_done, 1)
                        dve.wait_ge(d_ok_done, t + 1)
                        nc.vector.tensor_reduce(count[:], d_mask, AX_X, ALU.add).then_inc(d_cnt_done, 1)
                    nc.vector.tensor_scalar(d_neg, d_mask, big, -big, ALU.mult, ALU.add).then_inc(d_neg_done, 1)
                    nc.vector.tensor_scalar(d_score, d_t, row[:, 0, X_S:X_S + 1], None, ALU.add).then_inc(e1_done, 1)
                    dve.wait_ge(e1_done, g + 1)
                    nc.vector.scalar_tensor_tensor(out=d_score, in0=d_score, scalar=SLOPE, in1=d_score,
                                                   op0=ALU.mult, op1=ALU.max).then_inc(e2_done, 1)
                    dve.wait_ge(e2_done, g + 1)
                    if l < 2:
                        nc.vector.tensor_tensor(d_score, d_score, d_mask, ALU.mult).then_inc(gw_done, 1)
                        dve.wait_ge(gw_done, g + 1)
                    dve.wait_ge(d_neg_done, g + 1)
                    nc.vector.tensor_tensor(d_score, d_score, d_neg, ALU.add).then_inc(d_add_done, 1)
                    dve.wait_ge(d_add_done, g + 1)
                    nc.vector.tensor_reduce(emax[:], d_score, AX_X, ALU.max).then_inc(emax_done, 1)
                    dve.wait_ge(emax_done, g + 1)
                    nc.vector.tensor_scalar(nemax[:, 0:1], emax[:], -1.0, None, ALU.mult).then_inc(nemax_done, 1)
                    nc.vector.memset(agg[:], 0.0).then_inc(d_clear_done, 1)
                    dve.wait_ge(prob_done, g + 1)
                    nc.vector.reciprocal(rsum[:], psum_p[:, 0:1]).then_inc(rsum_done, 1)
                    dve.wait_ge(rsum_done, g + 1)
                    factor = rsum
                    if l == 1:
                        nc.vector.scalar_tensor_tensor(out=d_score, in0=d_score, scalar=rsum[:], in1=d_mask,
                                                       op0=ALU.mult, op1=ALU.mult).then_inc(share_done, 1)
                        dve.wait_ge(share_done, t + 1)
                        nc.vector.tensor_reduce(top[:], d_score, AX_X, ALU.max).then_inc(top_done, 1)
                        dve.wait_ge(top_done, t + 1)
                        nc.vector.scalar_tensor_tensor(out=d_score, in0=d_score, scalar=THR, in1=d_score,
                                                       op0=ALU.is_ge, op1=ALU.mult).then_inc(wgt_done, 1)
                        dve.wait_ge(d_cnt_done, t + 1)
                        nc.vector.tensor_scalar(fac[:], top[:], THR, count[:], ALU.is_gt, ALU.mult).then_inc(fac_done, 1)
                        dve.wait_ge(wgt_done, t + 1)
                        dve.wait_ge(fac_done, t + 1)
                        factor = fac
                    dve.wait_ge(d_clear_done, g + 1)
                    dve.sem_inc(passed, 1)
                    with dve.Fori(0, T) as c:
                        q = g * T + c
                        nc.vector.tensor_copy(d_part, d_score[:, bass.ds(c * P, P)]).then_inc(d_part_done, 1)
                        dve.wait_ge(d_mm_done, q + 1)
                        nc.vector.tensor_tensor(agg[:], agg[:], hw_ps[:, 0, 0:F], ALU.add).then_inc(d_acc_done, 1)
                        dve.wait_ge(d_acc_done, q + 1)
                        dve.sem_inc(passed, 1)
                    x_row = row[:, 0, 0:F]
                    if l == 2:
                        nc.vector.scalar_tensor_tensor(out=new[:, 0, 0:F], in0=agg[:], scalar=factor[:], in1=x_row,
                                                       op0=ALU.mult, op1=ALU.add).then_inc(x_new, 1)
                    else:
                        elu_residual(dve, g, 0, l, factor, x_row)
                    dve.wait_ge(x_new, g + 1)
                    node_dve_stats(dve, 0, m, new[:, 0, 0:F])
                    node_dve_norm(dve, 0, m, new[:, 0, 0:F])
                    if l == 0:
                        mark_unattendable(dve, 0, t)
                    dve.wait_ge(d_kept_out, 16 * (g + 1))
                    dve.wait_ge(d_tab_out, 16 * (g + 1))
                    dve.sem_inc(passed, 1)
            dve.wait_ge(d_turn_done, 3 * T * T + T)
            with dve.Fori(0, N) as i:
                dve.wait_ge(d_row_in, 16 * (i + 1))
                nc.vector.tensor_scalar(d_mask, d_adj, 0.0, None, ALU.not_equal).then_inc(d_rmask_done, 1)
                dve.wait_ge(d_rmask_done, i + 1)
                nc.vector.tensor_tensor(d_neg, d_score, d_mask, ALU.mult).then_inc(d_prod_done, 1)
                dve.wait_ge(d_prod_done, i + 1)
                nc.vector.tensor_reduce(emax[:], d_neg, AX_X, ALU.max).then_inc(d_max_done, 1)
                dve.wait_ge(d_max_done, i + 1)
                nc.vector.tensor_scalar(d_t[:, bass.ds(i, 1)], emax[:], 1.0, None, ALU.mult).then_inc(d_col_done, 1)
            dve.wait_ge(d_col_done, N)
            with dve.Fori(0, T) as t:
                q = 3 * T * T + t
                nc.vector.tensor_copy(d_part, d_t[:, bass.ds(t * P, P)]).then_inc(d_part_done, 1)
                dve.wait_ge(d_partT_done, q + T + 1)
                dve.wait_ge(d_in, 48 * 3 * T + 16 * (t + 1))
                nc.vector.tensor_tensor(new[:, 0, 0:F], hT_ps[:, 0, 0:P], row[:, 0, 0:F], ALU.add).then_inc(x_new, 1)
                dve.wait_ge(d_out, 16 * (t + 1))
                dve.sem_inc(passed, 1)

        def elu_residual(dve, g, b, l, factor, x_row):
            if l == 0:
                nc.vector.tensor_scalar(z[:, b, :], agg[:], factor[:], None, ALU.mult).then_inc(z_done, 1)
            else:
                nc.vector.scalar_tensor_tensor(out=z[:, b, :], in0=agg[:], scalar=factor[:], in1=row[:, b, F:2 * F],
                                               op0=ALU.mult, op1=ALU.add).then_inc(z_done, 1)
            dve.wait_ge(z_done, g + 1)
            nc.vector.tensor_scalar(zneg[:, b, :], z[:, b, :], 0.0, None, ALU.min).then_inc(zneg_done, 1)
            dve.wait_ge(ez_done, g + 1)
            nc.vector.scalar_tensor_tensor(out=z1[:], in0=z[:, b, :], scalar=0.0, in1=ez[:, b, :],
                                           op0=ALU.max, op1=ALU.add).then_inc(z1_done, 1)
            dve.wait_ge(z1_done, g + 1)
            nc.vector.scalar_tensor_tensor(out=new[:, b, 0:F], in0=z1[:], scalar=-1.0, in1=x_row,
                                           op0=ALU.add, op1=ALU.add).then_inc(x_new, 1)

        def mark_unattendable(dve, b, t):
            dve.wait_ge(row_done, rows_after(1, t))
            nc.vector.tensor_scalar(hzero[:], hsum[:, b:b + 1], 0.0, FAR, ALU.is_equal, ALU.mult).then_inc(hzero_done, 1)
            dve.wait_ge(hzero_done, t + 1)
            nc.vector.tensor_tensor(new[:, b, X_T:X_T + 1], new[:, b, X_T:X_T + 1], hzero[:],
                                    ALU.add).then_inc(tflag_done, 1)

        @block.sync
        def _(sp):
            sp.dma_start(w_sb[0][:], w0).then_inc(w_in, 16)
            sp.dma_start(w_sb[1][:], w1).then_inc(w_in, 16)
            for l, a in enumerate((a0, a1, a2)):
                sp.dma_start(att[l][:, 0:1], a[F:2 * F, :]).then_inc(w_in, 16)
                sp.dma_start(att[l][:, 1:2], a[0:F, :]).then_inc(w_in, 16)

            def load_adj(t, b):
                sp.dma_start(adj_t[:, b, :], rows_of(adj, t)).then_inc(adj_in[b], 16)

            def load_x(t, b):
                sp.dma_start(new[:, b, 0:F], rows_of(x, t)).then_inc(x_in[b], 16)
                sp.dma_start(rec[:, t, R_X:RW], rows_of(x, t)).then_inc(recx_in, 16)

            load_adj(0, 0)
            load_x(0, 0)
            load_adj(1, 1)
            for first, last in ((0, 1), (1, PAIRS - 1)):
                for i in pairs_of(sp, first, last) if last > first else ():
                    for b in range(2):
                        t = 2 * i + b
                        sp.wait_ge(sq_done, t + 1)
                        sp.sem_inc(passed, 1)
                        load_adj(t + 2, b)
                        at_least(sp, xn_done, t)
                        sp.sem_inc(passed, 1)
                        load_x(t + 1, 1 - b)
            sp.wait_ge(xn_done, T - 2)
            load_x(T - 1, 1)
            sp.wait_ge(verdict_done, 1)
            v = sp.value_load(verdict[0:1, 0:1], min_val=0, max_val=2 ** 30)
            with sp.If(v < 1):
                sp.wait_ge(sorted_out, 16 * T)
                for l in range(LAYERS):
                    if l:
                        for b in range(2):
                            sp.wait_ge(kept_out[b], 16 * PAIRS * l)

                    def load_tile(t, b):
                        sp.dma_start(idx[b][:], rows_of(srt.bitcast(U32)[:, 0:R_S], t)).then_inc(idx_in[b], 16)

                    def load_row(t, b):
                        if l:
                            sp.dma_start(row[:, b, :], rows_of(kept[l], t)).then_inc(row_in[b], 16)
                        else:
                            sp.dma_start(row[:, b, 0:F], rows_of(srt[:, R_X:RW], t)).then_inc(row_in[b], 16)
                            sp.dma_start(row[:, b, X_S:X_S + 2], rows_of(srt[:, R_S:R_S + 2], t)).then_inc(row_in[b], 16)

                    for b in range(2):
                        if l:
                            sp.wait_ge(g_in[b], 16 * gathers(l, 0, 0, 0))
                            sp.wait_ge(rid_done, T * l)
                            sp.wait_ge(x_new, T * l)
                        load_tile(b, b)
                        load_row(b, b)
                    for first, last, cap in groups:
                        for i in pairs_of(sp, first, min(last, PAIRS - 1)) if first < PAIRS - 1 else ():
                            for b in range(2):
                                g = T * l + 2 * i + b
                                sp.wait_ge(g_in[b], 16 * gathers(l, first, i + 1, cap))
                                sp.sem_inc(passed, 1)
                                sp.wait_ge(rid_done, g + 1)
                                sp.sem_inc(passed, 1)
                                load_tile(2 * i + b + 2, b)
                                sp.wait_ge(x_new, g + 1)
                                sp.sem_inc(passed, 1)
                                load_row(2 * i + b + 2, b)

            with sp.Else():
                dense_loads(sp)

        @block.gpsimd
        def _(pool):
            nc.gpsimd.iota(pos[:], [[1, BLK]], base=1, channel_multiplier=0,
                           allow_small_or_imprecise_dtypes=True).then_inc(const_pool, 1)
            nc.gpsimd.iota(blk_base[:], [[BLK, NBLK], [0, TOP]], base=0, channel_multiplier=0,
                           allow_small_or_imprecise_dtypes=True).then_inc(const_pool, 1)
            nc.gpsimd.iota(cls[:], [[-1, C]], base=DMAX, channel_multiplier=0,
                           allow_small_or_imprecise_dtypes=True).then_inc(const_pool, 1)
            nc.gpsimd.iota(node[:, :, 0], [[P, T]], base=1, channel_multiplier=1).then_inc(const_pool, 1)
            nc.gpsimd.iota(node[:, :, 1], [[P, T]], base=0, channel_multiplier=1).then_inc(const_pool, 1)
            nc.gpsimd.iota(node_f[:], [[P, T]], base=1, channel_multiplier=1,
                           allow_small_or_imprecise_dtypes=True).then_inc(const_pool, 1)
            nc.gpsimd.memset(ones_f[:], 1.0).then_inc(const_pool, 1)
            nc.gpsimd.memset(ones_b[:], 1.0).then_inc(const_pool, 1)
            nc.gpsimd.memset(eps[:], EPS).then_inc(const_pool, 1)
            pool.wait_ge(const_pool, 9)
            nc.gpsimd.affine_select(out=ident[:], in_=ones_f[:], compare_op=ALU.is_equal, fill=0.0, base=0,
                                    pattern=[[-1, P]], channel_multiplier=1).then_inc(const_pool, 1)
            nc.gpsimd.affine_select(out=tri[:], in_=ones_b[:], compare_op=ALU.is_gt, fill=0.0, base=0,
                                    pattern=[[1, P]], channel_multiplier=-1).then_inc(const_pool, 1)
            with pool.Fori(0, PAIRS) as i:
                for b in range(2):
                    pool.wait_ge(sq_done, 2 * i + b + 1)
                    part = sq[b][:, 0:POOL_BLK * BLK].rearrange("p (n w) -> p n w", w=BLK)
                    nc.gpsimd.tensor_tensor(part, part, pos[:, None, :].broadcast_to([P, POOL_BLK, BLK]),
                                            ALU.mult).then_inc(key_pool, 1)
            pool.wait_ge(verdict_done, 1)
            v = pool.value_load(verdict[0:1, 0:1], min_val=0, max_val=2 ** 30)
            with pool.If(v < 1):
                pool.wait_ge(recx_in, 16 * T)
                pool.wait_ge(s_kept, 3 * T)
                for t in range(T):
                    nc.gpsimd.indirect_dma_start(srt, bass.IndirectOffsetOnAxis(rank_u[:, t:t + 1], 0),
                                                 rec[:, t, :], None).then_inc(sorted_out, 16)
                for b in range(2):
                    pool.wait_ge(tab_nat[b], 16 * PAIRS)
                pool.wait_ge(dummy_out, 16 * LAYERS)
                for l in range(LAYERS):
                    if l:
                        for b in range(2):
                            pool.wait_ge(tab_out[b], 16 * PAIRS * l)

                    def scatter(t, b):
                        if l < 3:
                            if l == 0:
                                pool.wait_ge(tflag_done, t + 1)
                            elif l == 1:
                                pool.wait_ge(row_done, rows_after(2, t))
                            else:
                                pool.wait_ge(hn_done, 3 * T + t + 1)
                            pool.sem_inc(passed, 1)
                            nc.gpsimd.indirect_dma_start(table[l + 1], bass.IndirectOffsetOnAxis(rid[b][:, 0:1], 0),
                                                         new[:, b, F:XW], None).then_inc(tab_out[b], 16)
                        else:
                            pool.wait_ge(rid_done, T * l + t + 1)
                            pool.wait_ge(x_new, T * l + t + 1)
                            pool.sem_inc(passed, 1)
                            nc.gpsimd.indirect_dma_start(out, bass.IndirectOffsetOnAxis(rid[b][:, 1:2], 0),
                                                         new[:, b, 0:F], None).then_inc(res_out[b], 16)

                    for first, last, cap in groups:
                        for i in pairs_of(pool, first, last):
                            for b in range(2):
                                g = T * l + 2 * i + b
                                pool.wait_ge(idx_in[b], 16 * (PAIRS * l + i + 1))
                                at_least(pool, agg_done, g - 1)
                                pool.sem_inc(passed, 1)
                                for k in [*range(cap), R_TAB][:cap + (l == 0)]:
                                    nc.gpsimd.indirect_dma_start(
                                        gath[b][:, min(k, cap), :], None, table[l],
                                        bass.IndirectOffsetOnAxis(idx[b][:, k:k + 1], 0)).then_inc(g_in[b], 16)
                                if first or b:
                                    scatter(2 * i + b - 1, 1 - b)
                    scatter(T - 1, 1)
                for b in range(2):
                    pool.wait_ge(res_out[b], 16 * PAIRS)
                    pool.wait_ge(tab_out[b], 16 * PAIRS * 3)

        @block.scalar
        def _(act):
            for l in range(2):
                act.wait_ge(wT_ps, l + 1)
                nc.scalar.activation(wT[l][:], hT_ps[:, l, 0:P], ACT.Copy).then_inc(wT_sb, 1)
            for l in range(2):
                act.wait_ge(wa_ps, l + 1)
                nc.scalar.activation(wx[l][:, 0:F], w_sb[l][:], ACT.Copy).then_inc(wx_done, 1)
                nc.scalar.activation(wx[l][:, F:F + 2], hw_ps[:, l, 0:2], ACT.Copy).then_inc(wx_done, 1)
            act.wait_ge(dummy_set, 2)
            act.wait_ge(const_dve, 1)
            for l in range(LAYERS):
                act.dma_start(table[l][0:1, :], no_row[:]).then_inc(dummy_out, 16)
            act.wait_ge(const_pool, 11)

            def square(t, b):
                nc.scalar.activation(sq[b][:], adj_t[:, b, :], ACT.Square,
                                     accum_out=squares[:, bass.ds(t, 1)]).then_inc(sq_done, 1)

            def keep_list(t, b):
                act.wait_ge(deg_done, t + 1)
                act.sem_inc(passed, 1)
                nc.scalar.activation(rec[:, t, 0:KMAX].bitcast(U32), lst[:, b, :], ACT.Copy).then_inc(lst_free, 1)
                nc.scalar.activation(rec[:, t, R_TAB:R_S].bitcast(U32), node[:, t, :], ACT.Copy).then_inc(s_kept, 1)
                nc.scalar.activation(rec[:, t, R_S + 1:R_X], eps[:], ACT.Copy).then_inc(s_kept, 1)

            def rows(i, b):
                t = 2 * i + b

                def table_row_left():
                    at_least(act, tab_nat[b], 16 * i)
                node_act(act, b, t, 0, table_row_left)
                act.wait_ge(row_done, 2 * (t + 1))
                act.dma_start(rows_of(table[0], t, 1), new[:, b, F:XW]).then_inc(tab_nat[b], 16)
                act.sem_inc(passed, 1)
                nc.scalar.activation(rec[:, t, R_S:R_S + 1], new[:, b, X_S:X_S + 1], ACT.Copy).then_inc(s_kept, 1)

            def natural(i, b):
                t = 2 * i + b
                if not (isinstance(t, int) and t == T - 1):
                    act.wait_ge(adj_in[1 - b], 16 * (i + 1 + b))
                    at_least(act, max_done, t)
                    act.sem_inc(passed, 1)
                    square(t + 1, 1 - b)
                node_act_std(act, b, t)
                if not (isinstance(t, int) and t == 0):
                    rows(i - 1 + b, 1 - b)
                if b == 0 and not (isinstance(i, int) and i == 0):
                    for c in range(2):
                        keep_list(2 * (i - 1) + c, c)

            act.wait_ge(adj_in[0], 16)
            square(0, 0)
            for first, last in ((0, 1), (1, PAIRS - 1), (PAIRS - 1, PAIRS)):
                for i in pairs_of(act, first, last) if last > first else ():
                    for b in range(2):
                        natural(i, b)
            rows(PAIRS - 1, 1)
            for c in range(2):
                keep_list(T - 2 + c, c)
            act.wait_ge(verdict_done, 1)
            v = act.value_load(verdict[0:1, 0:1], min_val=0, max_val=2 ** 30)
            with act.If(v < 1):
                for l in range(LAYERS):
                    for first, last, cap in groups:
                        for i in pairs_of(act, first, last):
                            for b in range(2):
                                t = 2 * i + b
                                g = T * l + t
                                act.wait_ge(idx_in[b], 16 * (PAIRS * l + i + 1))
                                at_least(act, tab_out[b], 16 * (PAIRS * min(l, 3) + i) if l < 3 else 16 * PAIRS * 3)
                                if l == 3:
                                    at_least(act, res_out[b], 16 * i)
                                nc.scalar.activation(rid[b][:], idx[b][:, R_TAB:R_S], ACT.Copy).then_inc(rid_done, 1)
                                if l:
                                    act.wait_ge(row_in[b], rows_in(l, i))
                                    act.wait_ge(agg_done, g - 1)
                                    nc.scalar.activation(gath[b][:, cap, :], row[:, b, F:XW], ACT.Copy).then_inc(own_done, 1)
                                if l < 3:
                                    act.wait_ge(nemax_done, g + 1)
                                    kw = {} if l == 1 else {"accum_out": psum_p[:, b:b + 1]}
                                    nc.scalar.activation(prob[:, b, 0:cap + 1], e2[:, b, 0:cap + 1], ACT.Exp,
                                                         bias=nemax[:, b:b + 1], **kw).then_inc(prob_done, 1)
                                if l < 2:
                                    act.wait_ge(zneg_done, g + 1)
                                    nc.scalar.activation(ez[:, b, :], zneg[:, b, :], ACT.Exp).then_inc(ez_done, 1)
                                if l < 3:
                                    def kept_left():
                                        at_least(act, kept_out[b], 16 * (PAIRS * l + i))
                                    node_act_std(act, b, g + T)
                                    node_act(act, b, g + T, l + 1, kept_left)
                                    if l == 0:
                                        act.wait_ge(tflag_done, t + 1)
                                    if l == 1:
                                        act.wait_ge(row_done, rows_after(2, t))
                                    if l == 2:
                                        act.wait_ge(hn_done, g + T + 1)
                                    act.dma_start(rows_of(kept[l + 1], t), new[:, b, :]).then_inc(kept_out[b], 16)
                for b in range(2):
                    act.wait_ge(kept_out[b], 16 * PAIRS * 3)
            with act.Else():
                dense_act(act)

        @block.tensor
        def _(pe):
            pe.wait_ge(w_in, 16 * 8)
            pe.wait_ge(const_pool, 11)
            for l in range(2):
                nc.tensor.transpose(hT_ps[:, l, 0:P], w_sb[l][:], ident[:]).then_inc(wT_ps, 1)
            for l in range(2):
                pe.wait_ge(wT_sb, l + 1)
                nc.tensor.matmul(hw_ps[:, l, 0:2], wT[l][:], att[l][:], start=True, stop=True).then_inc(wa_ps, 1)
            pe.wait_ge(wx_done, 4)
            with pe.Fori(0, PAIRS) as i:
                for b in range(2):
                    node_pe(pe, b, 2 * i + b, 0)
            pe.wait_ge(dv, 1)
            pe.wait_ge(row_done, 2 * T)
            for c0, c1 in CT_CHUNKS:
                last = nc.tensor.matmul(rank_ps[:, c0:c1], ones_b[:], eq[:, c0:c1], start=True, stop=True)
            last.then_inc(tot_ps, 1)
            pe.wait_ge(tot_sb, 1)
            for c0, c1 in CT_CHUNKS:
                last = nc.tensor.matmul(rank_ps[:, c0:c1], tri[:], eq[:, c0:c1], start=True, stop=True)
            last.then_inc(tri_ps, 1)
            pe.wait_ge(bad_ps, 1)
            nc.tensor.matmul(hw_ps[:, 0, 0:1], ones_f[:], bad_sum[:], start=True, stop=True).then_inc(bad_ps, 1)
            pe.wait_ge(verdict_done, 1)
            v = pe.value_load(verdict[0:1, 0:1], min_val=0, max_val=2 ** 30)
            with pe.If(v < 1):
                for l in range(2):
                    with pe.Fori(0, PAIRS) as i:
                        for b in range(2):
                            node_pe(pe, b, T * (l + 1) + 2 * i + b, l + 1)
            with pe.Else():
                dense_pe(pe)

        @block.vector
        def _(dve):
            nc.vector.memset(no_row[:], 0.0).then_inc(dummy_set, 1)
            dve.wait_ge(dummy_set, 1)
            nc.vector.memset(no_row[:, F:F + 1], FAR).then_inc(dummy_set, 1)
            nc.vector.memset(new[:, :, F:XW], 0.0).then_inc(const_dve, 1)
            for c in range(C):
                fits = sum(2 * P for cap in CAPS if cap >= DMAX - c)
                nc.vector.memset(limit[:, c:c + 1], float(fits)).then_inc(const_dve, 1)
            dve.wait_ge(const_dve, C + 1)
            dve.wait_ge(const_pool, 11)

            def search(t, b):
                dve.wait_ge(sq_done, t + 1)
                part = sq[b][:, POOL_BLK * BLK:N].rearrange("p (n w) -> p n w", w=BLK)
                nc.vector.tensor_tensor(part, part, pos[:, None, :].broadcast_to([P, NBLK - POOL_BLK, BLK]),
                                        ALU.mult).then_inc(key_dve, 1)
                dve.wait_ge(key_dve, t + 1)
                dve.wait_ge(key_pool, t + 1)
                dve.sem_inc(passed, 1)
                for n in range(NBLK):
                    last = nc.vector.max(cand[:, b, n, :], sq[b][:, n * BLK:(n + 1) * BLK])
                last.then_inc(max_done, 1)

            def lists(i):
                both = [(b, 2 * i + b) for b in range(2)]
                for b, t in both:
                    dve.wait_ge(max_done, t + 1)
                    nc.vector.tensor_tensor(cand_b[:, b], cand[:, b], blk_base[:], ALU.add).then_inc(cb_done, 1)
                for b, t in both:
                    dve.wait_ge(cb_done, t + 1)
                    nc.vector.scalar_tensor_tensor(
                        out=cand_g[:, b, :], in0=cand[:, b].rearrange("p n k -> p (n k)"), scalar=0.0,
                        in1=cand_b[:, b].rearrange("p n k -> p (n k)"), op0=ALU.is_gt, op1=ALU.mult).then_inc(cg_done, 1)
                for b, t in both:
                    dve.wait_ge(cg_done, t + 1)
                    nc.vector.scalar_tensor_tensor(out=cand_g[:, b, :], in0=cand_g[:, b, :], scalar=node_f[:, bass.ds(t, 1)],
                                                   in1=cand_g[:, b, :], op0=ALU.not_equal, op1=ALU.mult).then_inc(self_out, 1)
                at_least(dve, lst_free, 2 * i)
                ROUNDS = KMAX // TOP
                for r in range(ROUNDS):
                    for b, t in both:
                        if r:
                            dve.wait_ge(round_done[b], (2 * ROUNDS - 1) * i + 2 * r)
                        else:
                            dve.wait_ge(self_out, t + 1)
                        dve.sem_inc(passed, 1)
                        nc.vector.max(lst[:, b, r * TOP:(r + 1) * TOP], cand_g[:, b, :]).then_inc(round_done[b], 1)
                    for b, t in both:
                        if r < ROUNDS - 1:
                            dve.wait_ge(round_done[b], (2 * ROUNDS - 1) * i + 2 * r + 1)
                            dve.sem_inc(passed, 1)
                            nc.vector.match_replace(cand_g[:, b, :], lst[:, b, r * TOP:(r + 1) * TOP],
                                                    cand_g[:, b, :], 0.0).then_inc(round_done[b], 1)
                for b, t in both:
                    dve.wait_ge(round_done[b], (2 * ROUNDS - 1) * (i + 1))
                    nc.vector.tensor_scalar(lst_c[:, b, :], lst[:, b, :], 0.0, 0.0, ALU.is_gt, ALU.add,
                                            accum_out=deg[:, bass.ds(t, 1)]).then_inc(deg_done, 1)

            for first, last in ((0, 1), (1, PAIRS)):
                for i in pairs_of(dve, first, last):
                    for b in range(2):
                        t = 2 * i + b
                        dve.wait_ge(x_in[b], 16 * (i + 1))
                        node_dve_stats(dve, b, t, new[:, b, 0:F])
                        search(t, b)
                        node_dve_norm(dve, b, t, new[:, b, 0:F])
                    lists(i)

            steps = [0]

            def step(ins):
                steps[0] += 1
                ins.then_inc(dv, 1)
                dve.wait_ge(dv, steps[0])

            def by_class(t):
                return t.rearrange("p (c t) -> p c t", c=C)

            dve.wait_ge(deg_done, T)
            step(nc.vector.tensor_tensor(by_class(eq[:]), deg[:, None, :].broadcast_to([P, C, T]),
                                         cls[:, :, None].broadcast_to([P, C, T]), ALU.is_equal))
            step(nc.vector.memset(ones_ct, 1.0))
            dve.wait_ge(tot_ps, 1)
            nc.vector.tensor_copy(totals, rank_ps[:, 0:CT]).then_inc(tot_sb, 1)
            dve.wait_ge(tot_sb, 1)
            step(nc.vector.tensor_tensor_scan(scan, ones_ct, totals, 0.0, ALU.mult, ALU.add))
            step(nc.vector.tensor_tensor(scan, scan, totals, ALU.subtract))
            dve.wait_ge(tri_ps, 1)
            step(nc.vector.tensor_tensor(value, rank_ps[:, 0:CT], scan, ALU.add))
            step(nc.vector.tensor_tensor(value, value, eq[:], ALU.mult))
            step(nc.vector.tensor_reduce(rank[:], by_class(value).rearrange("p c t -> p t c"), AX_X, ALU.add))
            step(nc.vector.tensor_copy(rank_u[:], rank[:]))
            step(nc.vector.tensor_tensor(by_class(totals), by_class(value),
                                         limit[:, :, None].broadcast_to([P, C, T]), ALU.is_ge))
            step(nc.vector.tensor_reduce(bad[:, 0:1], totals, AX_X, ALU.add))
            dve.wait_ge(sq_done, T)
            step(nc.vector.scalar_tensor_tensor(out=flags[:], in0=deg[:], scalar=1.0, in1=squares[:],
                                                op0=ALU.add, op1=ALU.not_equal))
            step(nc.vector.tensor_reduce(bad[:, 1:2], flags[:], AX_X, ALU.add))
            step(nc.vector.tensor_scalar(flags[:], deg[:], float(DMAX), None, ALU.is_gt))
            step(nc.vector.tensor_reduce(bad[:, 2:3], flags[:], AX_X, ALU.add))
            step(nc.vector.tensor_reduce(bad_sum[:], bad[:, 0:3], AX_X, ALU.add))
            nc.vector.sem_inc(bad_ps, 1)
            dve.wait_ge(bad_ps, 2)
            nc.vector.tensor_copy(verdict[:], hw_ps[:, 0, 0:1]).then_inc(verdict_done, 1)
            dve.wait_ge(verdict_done, 1)
            v = dve.value_load(verdict[0:1, 0:1], min_val=0, max_val=2 ** 30)

            def layer_tile(l, i, b, cap, first):
                t = 2 * i + b
                g = T * l + t
                cap = cap + 1
                G = gath[b][:, 0:cap, :]
                feats = G[:, :, 0:F]
                dve.wait_ge(row_in[b], rows_in(l, i))
                dve.wait_ge(g_in[b], 16 * gathers(l, first, i + 1, cap - 1))
                if l:
                    dve.wait_ge(own_done, g - T + 1)
                if l < 3:
                    nc.vector.tensor_scalar(e1[:, 0:cap], G[:, :, F], row[:, b, X_S:X_S + 1], None,
                                            ALU.add).then_inc(e1_done, 1)
                    dve.wait_ge(e1_done, g + 1)
                    nc.vector.scalar_tensor_tensor(out=e2[:, b, 0:cap], in0=e1[:, 0:cap], scalar=SLOPE,
                                                   in1=e1[:, 0:cap], op0=ALU.mult, op1=ALU.max).then_inc(e2_done, 1)
                    dve.wait_ge(e2_done, g + 1)
                    nc.vector.tensor_reduce(emax[:], e2[:, b, 0:cap], AX_X, ALU.max).then_inc(emax_done, 1)
                    dve.wait_ge(emax_done, g + 1)
                    nc.vector.tensor_scalar(nemax[:, b:b + 1], emax[:], -1.0, None, ALU.mult).then_inc(nemax_done, 1)
                    weights = prob[:, b, 0:cap]
                if l in (0, 2):
                    dve.wait_ge(prob_done, g + 1)
                    nc.vector.reciprocal(rsum[:], psum_p[:, b:b + 1]).then_inc(rsum_done, 1)
                    factor, ready = rsum, (rsum_done, g + 1)
                if l == 1:
                    nc.vector.tensor_scalar(ok[:, 0:cap], G[:, :, F], FAR / 10, 0.0, ALU.is_gt, ALU.add,
                                            accum_out=count[:]).then_inc(ok_done, 1)
                    dve.wait_ge(ok_done, t + 1)
                    dve.wait_ge(prob_done, g + 1)
                    nc.vector.scalar_tensor_tensor(out=pok[:, 0:cap], in0=prob[:, b, 0:cap], scalar=1.0,
                                                   in1=ok[:, 0:cap], op0=ALU.mult, op1=ALU.mult,
                                                   accum_out=sums[:]).then_inc(pok_done, 1)
                    dve.wait_ge(pok_done, t + 1)
                    nc.vector.tensor_scalar(top[:], sums[:], 1e-30, None, ALU.max).then_inc(sums_done, 1)
                    dve.wait_ge(sums_done, t + 1)
                    nc.vector.reciprocal(rsum[:], top[:]).then_inc(rsum_done, 1)
                    dve.wait_ge(rsum_done, g + 1)
                    nc.vector.tensor_scalar(share[:, 0:cap], pok[:, 0:cap], rsum[:], None, ALU.mult).then_inc(share_done, 1)
                    dve.wait_ge(share_done, t + 1)
                    nc.vector.tensor_reduce(top[:], share[:, 0:cap], AX_X, ALU.max).then_inc(top_done, 1)
                    nc.vector.scalar_tensor_tensor(out=wgt[:, 0:cap], in0=share[:, 0:cap], scalar=THR,
                                                   in1=share[:, 0:cap], op0=ALU.is_ge, op1=ALU.mult).then_inc(wgt_done, 1)
                    dve.wait_ge(top_done, t + 1)
                    nc.vector.tensor_scalar(fac[:], top[:], THR, count[:], ALU.is_gt, ALU.mult).then_inc(fac_done, 1)
                    dve.wait_ge(wgt_done, t + 1)
                    weights = wgt[:, 0:cap]
                    factor, ready = fac, (fac_done, t + 1)
                if l < 3:
                    nc.vector.tensor_tensor(feats, feats, weights[:, :, None].broadcast_to([P, cap, F]),
                                            ALU.mult).then_inc(gw_done, 1)
                    dve.wait_ge(gw_done, g + 1)
                else:
                    dve.wait_ge(x_new, g)
                nc.vector.tensor_reduce(agg[:], feats.rearrange("p k f -> p f k"), AX_X,
                                        ALU.add if l < 3 else ALU.max).then_inc(agg_done, 1)
                dve.wait_ge(agg_done, g + 1)
                if l < 3:
                    dve.wait_ge(*ready)
                x_row = row[:, b, 0:F]
                if l < 3:
                    at_least(dve, kept_out[b], 16 * (PAIRS * l + i))
                elif not (first == 0):
                    dve.wait_ge(res_out[b], 16 * i)
                if l == 3:
                    if first == 0:
                        dve.wait_ge(kept_out[b], 16 * PAIRS * 3)
                    nc.vector.tensor_tensor(new[:, b, 0:F], agg[:], x_row, ALU.add).then_inc(x_new, 1)
                    return
                if l == 2:
                    nc.vector.scalar_tensor_tensor(out=new[:, b, 0:F], in0=agg[:], scalar=factor[:], in1=x_row,
                                                   op0=ALU.mult, op1=ALU.add).then_inc(x_new, 1)
                else:
                    elu_residual(dve, g, b, l, factor, x_row)
                dve.wait_ge(x_new, g + 1)
                m = g + T
                node_dve_stats(dve, b, m, new[:, b, 0:F])
                node_dve_norm(dve, b, m, new[:, b, 0:F])
                if l == 0:
                    mark_unattendable(dve, b, t)

            with dve.If(v < 1):
                for l in range(LAYERS):
                    for first, last, cap in groups:
                        for i in pairs_of(dve, first, last):
                            for b in range(2):
                                layer_tile(l, i, b, cap, first)
            with dve.Else():
                dense_dve(dve)


def kernel(x, adj, L0_gnn_W, L0_gnn_a, L1_gnn_W, L1_gnn_a, L2_gnn_attn):
    import numpy as np
    import concourse.bacc as bacc
    from concourse.bass_utils import run_bass_kernel_spmd

    given = {"x": x, "adj": adj, "w0": L0_gnn_W, "a0": L0_gnn_a, "w1": L1_gnn_W, "a1": L1_gnn_a, "a2": L2_gnn_attn}
    arrays = {name: np.ascontiguousarray(a) for name, a in given.items()}
    nc = bacc.Bacc("TRN2", target_bir_lowering=False, num_devices=1)
    args = [nc.dram_tensor(n, a.shape, mybir.dt.from_np(a.dtype), kind="ExternalInput").ap() for n, a in arrays.items()]
    out = nc.dram_tensor("out", x.shape, F32, kind="ExternalOutput").ap()
    build(nc, *args, out)
    r = run_bass_kernel_spmd(nc, [arrays], core_ids=[0])
    return r.results[0]["out"]
```

```python
from contextlib import ExitStack

import concourse.bass as bass
from concourse import mybir

ALU = mybir.AluOpType
ACT = mybir.ActivationFunctionType
F32 = mybir.dt.float32
BF16 = mybir.dt.bfloat16
I32 = mybir.dt.int32
U32 = mybir.dt.uint32
AX_X = mybir.AxisListType.X

P = 128
BLK = 256
TOP = 8
KMAX = 40
DMAX = KMAX - 1
EPS = 1e-5
SLOPE = 0.2
THR = 1e-4
NEG0 = 9000000000000000.0
NEG1 = 1000000000.0
FAR = -1e30
LAYERS = 4
EDGE_P = 1.0 - (1.0 - 0.000976562) ** 2

R_TAB, R_OUT, R_X = KMAX, KMAX + 1, KMAX + 2


def tile_capacities(n):
    pm = (1.0 - EDGE_P) ** (n - 1)
    at_most = []
    for k in range(1, KMAX + 1):
        at_most.append((at_most[-1] if at_most else 0.0) + pm)
        pm *= (n - k) / k * EDGE_P / (1.0 - EDGE_P)
    caps = []
    for first in range(0, n, P):
        cap = DMAX
        if first:
            for d in range(DMAX, 0, -1):
                above = max(n * (1.0 - at_most[d]), 0.0)
                if above + 4.0 * above ** 0.5 <= first:
                    cap = d
        caps.append(cap)
    return caps


def build(nc, x, adj, w0, a0, w1, a1, a2, out):
    N, F = x.shape
    T = N // P
    PAIRS = T // 2
    NBLK = N // BLK
    CAND = NBLK * TOP
    POOL_BLK = NBLK * 7 // 8
    RW = R_X + 2 * F + 2
    TW = F + 4
    XW = F + TW
    X_T, X_S = 2 * F, 2 * F + 1
    CAPS = tile_capacities(N)
    assert F == P and CAPS[0] == DMAX and N % BLK == 0

    ND = (T - 8) // 7
    TURNS = ND + 1
    SP_PAIRS = 3 * ND + 4
    assert T == 7 * ND + 8 and ND % 2 == 0 and T % 4 == 0 and ND > 0
    WIDE = 2

    groups = []
    pair_caps = [tuple(CAPS[2 * i:2 * i + 2]) for i in range(PAIRS)]
    for i, c in enumerate(pair_caps):
        if i > 1 and groups[-1][2] == c:
            groups[-1][1] = i + 1
        else:
            groups.append([i, i + 1, c])
    turn_caps = [tuple(CAPS[ND + 6 * k:ND + 6 * k + (6 if k < ND else 8)]) for k in range(TURNS)]
    turns = []
    for k, c in enumerate(turn_caps):
        if 2 < k < TURNS - 2 and turns[-1][2] == c:
            turns[-1][1] = k + 1
        else:
            turns.append([k, k + 1, c])
    pair_slots = [[sum(c[b] for c in pair_caps[:i]) for i in range(PAIRS + 1)] for b in range(2)]
    turn_slots = [[sum(sum(c[b::2]) for c in turn_caps[:k]) for k in range(TURNS + 1)] for b in range(2)]

    def uses(l, b):
        return l * (ND if b == WIDE else SP_PAIRS)

    class Tile:

        def __init__(self, l, t, b, u, n, cap=0, gathered=None):
            self.l, self.t, self.b, self.u, self.n, self.cap, self.gathered = l, t, b, u, n, cap, gathered
            self.g = T * l + n
            self.m = T + self.g
            self.used = uses(l, b) + u
            self.s = 2 * SP_PAIRS * l + 2 * u + b

    def gathered_tile(l, k, first, caps, j):
        b = j % 2
        u = 3 * k + j // 2
        slots = turn_slots[b][first] + (k - first) * sum(caps[b::2]) + sum(caps[b:j + 1:2])
        total = slots + l * turn_slots[b][-1]
        n = 7 * k + (j if j > 1 or first == 0 else j - 1)
        return Tile(l, ND + 2 * u + b, b, u, n, caps[j], total)

    def wide_tile(l, k):
        return Tile(l, k, WIDE, k, 7 * k + 8)

    def last_layer_tile(i, first, caps, b):
        return Tile(3, 2 * i + b, b, i, 2 * i + b, caps[b],
                    3 * turn_slots[b][-1] + pair_slots[b][first] + (i - first + 1) * caps[b])

    srt = nc.dram_tensor("sorted_records", [N, RW], F32).ap()
    kept = [None] + [nc.dram_tensor(f"kept{l}", [N, XW], F32).ap() for l in (1, 2, 3)]
    table = [nc.dram_tensor(f"table{l}", [N + 1, TW], F32).ap() for l in range(LAYERS)]

    with ExitStack() as ctx:
        def sb(name, shape, dt=F32):
            return ctx.enter_context(nc.sbuf_tensor(name, shape, dt))

        def sem(name):
            return ctx.enter_context(nc.semaphore(name))

        def sems(name, n=2):
            return [sem(f"{name}{b}") for b in range(n)]

        NG = KMAX * TW
        C = KMAX
        CT = C * T
        REGION = max(3 * N + T * RW, 4 * CT, 2 * NG + T * TW + 3 * N)
        region = sb("region", [P, REGION])

        def place(at, words):
            return region[:, at:at + words]
        adj_t = place(0, 2 * N).bitcast(I32).rearrange("p (b n) -> p b n", b=2)
        sq_all = place(2 * N, N).bitcast(BF16)
        sq = [sq_all[:, b * N:(b + 1) * N] for b in range(2)]
        rec_all = place(3 * N, T * RW)
        rec = rec_all.rearrange("p (t w) -> p t w", w=RW)
        gath = [place(b * NG, NG).rearrange("p (k w) -> p k w", w=TW) for b in range(2)]
        w_h = place(2 * NG, T * TW).rearrange("p (c w) -> p c w", w=TW)
        assert 2 * NG + T * TW <= 3 * N
        w_adj, w_e = (place(2 * NG + T * TW + i * N, N) for i in range(2))
        w_t = place(REGION - N, N)
        totals, scan, value, ones_ct = (place(i * CT, CT) for i in range(4))
        eq_or_turned = sb("eq_or_turned", [P, max(CT, 2048)], BF16)
        eq = eq_or_turned[:, 0:CT]
        deg = sb("deg", [P, T])
        squares = sb("squares", [P, T])
        plain = sb("plain", [P, T])
        rank = sb("rank", [P, T])
        rank_u = sb("rank_u", [P, T], U32)
        flags = sb("flags", [P, T])
        bad = sb("bad", [P, 4])
        bad_sum = sb("bad_sum", [P, 1])
        verdict = sb("verdict", [P, 1], I32)
        pos = sb("pos", [P, BLK], BF16)
        blk_base = sb("blk_base", [P, NBLK, TOP])
        cls = sb("cls", [P, C])
        limit = sb("limit", [P, C])
        tri = sb("tri", [P, P], BF16)
        ones_b = sb("ones_b", [P, P], BF16)
        ones_f = sb("ones_f", [P, P])
        ident = sb("ident", [P, P])
        node = sb("node", [P, T, 2], U32)
        node_f = sb("node_f", [P, T])
        eps = sb("eps", [P, 1])
        w_sb = [sb(f"w{l}_sb", [P, F]) for l in range(2)]
        att = [sb(f"att{l}", [P, 2]) for l in range(3)]
        wx = [sb(f"wx{l}", [P, F + 2]) for l in range(2)]
        no_row = sb("no_row", [1, TW])
        cand_or_z1 = sb("cand_or_z1", [P, max(2 * NBLK * TOP, 2 * F)], BF16)
        cand = cand_or_z1[:, 0:2 * NBLK * TOP].rearrange("p (b n k) -> p b n k", b=2, n=NBLK)
        cand_b_or_z = sb("cand_b_or_z", [P, max(2 * NBLK * TOP, 3 * F)])
        cand_b = cand_b_or_z[:, 0:2 * NBLK * TOP].rearrange("p (b n k) -> p b n k", b=2, n=NBLK)
        cand_g = sb("cand_g", [P, 2, CAND])
        lst = sb("lst", [P, 2, KMAX])
        lst_c = sb("lst_c", [P, 2, KMAX])
        stats = sb("stats", [P, 6])
        mv = sb("mv", [P, 3, 2])
        std = sb("std", [P, 3])
        rstd = sb("rstd", [P, 1])
        xn = sb("xn", [P, 3, F])
        hn = sb("hn", [P, 3, F])
        hnT = sb("hnT", [P, 3, F])
        new = sb("new", [P, 3, XW])
        hsum = sb("hsum", [P, 3])
        hzero = sb("hzero", [P, 1])
        idx = [sb(f"idx{b}", [P, R_X], U32) for b in range(3)]
        row = sb("row", [P, 3, XW])
        rid = [sb(f"rid{b}", [P, 2], U32) for b in range(3)]
        e1 = sb("e1", [P, KMAX])
        e2 = sb("e2", [P, 2, KMAX])
        emax = sb("emax", [P, 1])
        nemax = sb("nemax", [P, 2])
        prob = sb("prob", [P, 2, KMAX])
        psum_p = sb("psum_p", [P, 2])
        ok = sb("ok", [P, KMAX])
        count = sb("count", [P, 1])
        pok = sb("pok", [P, KMAX])
        sums = sb("sums", [P, 1])
        rsum = sb("rsum", [P, 1])
        share = sb("share", [P, KMAX])
        top = sb("top", [P, 1])
        wgt = sb("wgt", [P, KMAX])
        fac = sb("fac", [P, 1])
        agg = sb("agg", [P, F])
        w_tT = sb("w_tT", [T, P])
        w_s = sb("w_s", [P, 2])
        w_min, w_min1, w_max, w_s1, w_u, w_m = (sb(f"w_col{i}", [P, 1]) for i in range(6))
        w_us, w_negm, w_cnt, w_sum, w_rs, w_fac = (sb(f"w_col{i}", [P, 1]) for i in range(6, 12))
        w_mins, w_live, w_tile_min = rank, agg[0:T, :], w_u[0:T, :]
        w_eT = eq_or_turned[:, 0:2048].bitcast(F32).rearrange("p (a n) -> p a n", a=2)
        z = cand_b_or_z[:, 0:3 * F].rearrange("p (b f) -> p b f", b=3)
        zneg = sb("zneg", [P, 3, F])
        wT = [zneg[:, l, :] for l in range(2)]
        ez = sb("ez", [P, 3, F])
        z1 = cand_or_z1[:, 0:2 * F].bitcast(F32)

        banks = ctx.enter_context(nc.psum_tensor("banks", [P, 8, 512], F32))
        hT_ps = [banks[:, 0, 0:P], banks[:, 1, 0:P], banks[:, 7, 0:P]]
        hw_ps = [banks[:, 2, 0:256], banks[:, 3, 0:256], banks[:, 7, 256:512]]
        eT_ps, acc_ps = banks[:, 4:6, :], banks[:, 6, 0:F]
        rank_ps = banks[:, 3:8, :].rearrange("p b n -> p (b n)")
        assert CT <= 5 * 512
        CT_CHUNKS = [(c, min(c + 512, CT)) for c in range(0, CT, 512)]

        d_adj, d_neg, d_score = adj_t[:, 0, :], place(0, N), place(N, N)
        d_mask = rec_all.bitcast(BF16)[:, 0:N]
        d_t = place(2 * N, N)
        d_tcol, d_h, d_part = flags, ez[:, 1, :], z[:, 1, :]
        t_all = [nc.dram_tensor(f"t_all{l}", [T, P], F32).ap() for l in range(3)]
        t_min = [nc.dram_tensor(f"t_min{l}", [T, 1], F32).ap() for l in range(3)]

        const_pool, const_dve = sem("const_pool"), sem("const_dve")
        w_in, dummy_set, dummy_out = sem("w_in"), sem("dummy_set"), sem("dummy_out")
        wT_ps, wT_sb, wa_ps, wx_done = sem("wT_ps"), sem("wT_sb"), sem("wa_ps"), sem("wx_done")
        adj_in, x_in = sems("adj_in"), sems("x_in")
        recx_in = sem("recx_in")
        plain_done = sem("plain_done")
        sq_done, key_pool, key_dve = sem("sq_done"), sem("key_pool"), sem("key_dve")
        max_done, cb_done, cg_done = sem("max_done"), sem("cb_done"), sem("cg_done")
        round_done, lst_free = sems("round_done"), sem("lst_free")
        self_out = sem("self_out")
        own_done = sem("own_done")
        deg_done, passed = sem("deg_done"), sem("passed")
        st_done, mv_done, std_done, rstd_done = sem("st_done"), sem("mv_done"), sem("std_done"), sem("rstd_done")
        xn_done, hn_done, hT_done, hnT_done = sem("xn_done"), sem("hn_done"), sem("hT_done"), sem("hnT_done")
        hw_done, row_done = sem("hw_done"), sem("row_done")
        hzero_done, tflag_done = sem("hzero_done"), sem("tflag_done")
        s_kept = sem("s_kept")
        tab_nat = sems("tab_nat")
        w_ready, w_steps, w_rs_done, w_s1_done, w_s2_done, w_s3_done = (
            sem("w_ready"), sem("w_steps"), sem("w_rs_done"), sem("w_s1_done"), sem("w_s2_done"), sem("w_s3_done"))
        NQ = T // 4
        QUADS = {5: range(NQ // 3), 0: range(NQ // 3, 2 * NQ // 3), 1: range(2 * NQ // 3, NQ)}
        NDG = NQ * ND

        def scores_ready(x_):
            if x_.l == 1:
                return w_thr_done, x_.used - ND + 1
            return w_p_done, x_.used + 1

        dv, tot_ps, tot_sb, tri_ps, bad_ps, verdict_done = (
            sem("dv"), sem("tot_ps"), sem("tot_sb"), sem("tri_ps"), sem("bad_ps"), sem("verdict_done"))
        sorted_out = sem("sorted_out")
        idx_in, row_in, g_in = sems("idx_in", 3), sems("row_in", 3), sems("g_in")
        rid_done, x_new = sems("rid_done", 3), sem("x_new")
        e1_done, e2_done, emax_done, nemax_done, prob_done = (
            sem("e1_done"), sem("e2_done"), sem("emax_done"), sem("nemax_done"), sem("prob_done"))
        ok_done, pok_done, sums_done, share_done, top_done, wgt_done = (
            sem("ok_done"), sem("pok_done"), sem("sums_done"), sem("share_done"), sem("top_done"), sem("wgt_done"))
        rsum_done, fac_done, gw_done, z_done, zneg_done, ez_done, z1_done = (
            sem("rsum_done"), sem("fac_done"), sem("gw_done"), sem("z_done"),
            sem("zneg_done"), sem("ez_done"), sem("z1_done"))
        d_in, d_t_in, d_h_in, d_row_in = sem("d_in"), sem("d_t_in"), sem("d_h_in"), sem("d_row_in")
        d_mask_done, d_ok_done, d_neg_done, d_add_done = sem("d_mask_done"), sem("d_ok_done"), sem("d_neg_done"), sem("d_add_done")
        d_cnt_done, d_clear_done = sem("d_cnt_done"), sem("d_clear_done")
        d_part_done, d_partT_done, d_turn_done, d_mm_done, d_acc_done = (
            sem("d_part_done"), sem("d_partT_done"), sem("d_turn_done"), sem("d_mm_done"), sem("d_acc_done"))
        d_rmask_done, d_prod_done, d_max_done, d_col_done = (
            sem("d_rmask_done"), sem("d_prod_done"), sem("d_max_done"), sem("d_col_done"))
        d_kept_out, d_tab_out, d_out = sem("d_kept_out"), sem("d_tab_out"), sem("d_out")
        agg_done = sems("agg_done")
        kept_out, tab_out, res_out = sems("kept_out", 3), sems("tab_out", 3), sems("res_out")
        w_h_in, w_tT_ps, w_tT_sb, w_t_out, w_t_in = sem("w_h_in"), sem("w_tT_ps"), sem("w_tT_sb"), sem("w_t_out"), sem("w_t_in")
        w_live_done, w_min_done, w_prep = sem("w_live_done"), sem("w_min_done"), sem("w_prep")
        w_s_in = sem("w_s_in")
        w_adj_in, w_cols, w_max_done, w_m_done = sem("w_adj_in"), sem("w_cols"), sem("w_max_done"), sem("w_m_done")
        w_u_done, w_lrelu_done, w_exp_done = sem("w_u_done"), sem("w_lrelu_done"), sem("w_exp_done")
        w_p_done, w_thr_done, w_cnt_done, w_fac_done = sem("w_p_done"), sem("w_thr_done"), sem("w_cnt_done"), sem("w_fac_done")
        w_turned, w_copied, w_multiplied = sem("w_turned"), sem("w_copied"), sem("w_multiplied")

        block = ctx.enter_context(nc.Block())

        def at_least(eng, s, v):
            if not isinstance(v, int) or v > 0:
                eng.wait_ge(s, v)

        def pairs_of(eng, first, last):
            if last - first == 1:
                yield first
            else:
                with eng.Fori(first, last) as i:
                    yield i

        def rows_of(dram, tile, first=0):
            if isinstance(tile, int):
                return dram[tile * P + first:tile * P + first + P, :]
            return dram[bass.ds(tile * P + first, P), :]

        def node_dve_stats(dve, b, m, xin):
            nc.vector.bn_stats(stats[:], xin).then_inc(st_done, 1)
            dve.wait_ge(st_done, m + 1)
            dve.sem_inc(passed, 1)
            nc.vector.bn_aggr(mv[:, b, :], stats[:]).then_inc(mv_done, 1)

        def node_dve_norm(dve, b, m, xin):
            dve.wait_ge(std_done, m + 1)
            nc.vector.reciprocal(rstd[:], std[:, b:b + 1]).then_inc(rstd_done, 1)
            dve.wait_ge(rstd_done, m + 1)
            nc.vector.tensor_scalar(xn[:, b, :], xin, mv[:, b, 0:1], rstd[:], ALU.subtract, ALU.mult).then_inc(xn_done, 1)

        def node_act_std(act, b, m):
            act.wait_ge(mv_done, m + 1)
            nc.scalar.activation(std[:, b:b + 1], mv[:, b, 1:2], ACT.Sqrt, bias=eps[:]).then_inc(std_done, 1)

        def node_act(act, b, m, layer, scattered):
            h_row = new[:, b, F:2 * F]
            scattered()
            act.wait_ge(xn_done, m + 1)
            nc.scalar.activation(h_row if layer > 1 else hn[:, b, :], xn[:, b, :], ACT.Relu).then_inc(hn_done, 1)
            if layer == 3:
                return
            act.wait_ge(hT_done, m + 1)
            nc.scalar.activation(hnT[:, b, :], hT_ps[b], ACT.Copy).then_inc(hnT_done, 1)
            act.wait_ge(hw_done, m + 1)
            if layer == 2:
                nc.scalar.activation(new[:, b, X_T:X_T + 2], hw_ps[b][:, 0:2], ACT.Copy).then_inc(row_done, 1)
            else:
                nc.scalar.activation(h_row, hw_ps[b][:, 0:F], ACT.Copy, accum_out=hsum[:, b:b + 1]).then_inc(row_done, 1)
                nc.scalar.activation(new[:, b, X_T:X_T + 2], hw_ps[b][:, F:F + 2], ACT.Copy).then_inc(row_done, 1)

        def node_pe(pe, b, m, layer):
            if layer == 3:
                return
            h_in = new[:, b, F:2 * F] if layer == 2 else hn[:, b, :]
            pe.wait_ge(hn_done, m + 1)
            nc.tensor.transpose(hT_ps[b], h_in, ident[:]).then_inc(hT_done, 1)
            pe.wait_ge(hnT_done, m + 1)
            if layer == 2:
                nc.tensor.matmul(hw_ps[b][:, 0:2], hnT[:, b, :], att[2][:], start=True, stop=True).then_inc(hw_done, 1)
            else:
                nc.tensor.matmul(hw_ps[b][:, 0:F + 2], hnT[:, b, :], wx[layer][:], start=True, stop=True).then_inc(hw_done, 1)

        def rows_after(layer, t):
            return [2 * (t + 1), 2 * T + 2 * (t + 1), 4 * T + t + 1][layer]

        def row_sources(l, t):
            x_from = rows_of(x, t) if l == 0 else rows_of(kept[l][:, 0:F], t)
            return x_from, rows_of(table[l], t, 1)

        def dense_loads(sp):
            for l in range(3):
                if l:
                    sp.wait_ge(d_kept_out, 16 * T * l)
                    sp.wait_ge(d_tab_out, 16 * T * l)
                else:
                    for b in range(2):
                        sp.wait_ge(tab_nat[b], 16 * PAIRS)
                sp.dma_start(d_tcol[:, 0:T], table[l][1:N + 1, F:F + 1].rearrange("(t p) w -> p (t w)", p=P),
                             allow_slow_non_contiguous=True).then_inc(d_t_in, 16)
                sp.wait_ge(d_t_in, 48 * l + 16)
                sp.dma_start(t_all[l].rearrange("t p -> p t"), d_tcol[:, 0:T],
                             allow_slow_non_contiguous=True).then_inc(d_t_in, 16)
                sp.wait_ge(d_t_in, 48 * l + 32)
                sp.dma_start(d_t, t_all[l].rearrange("t p -> (t p)")[None, :].broadcast_to([P, N])).then_inc(d_t_in, 16)
                with sp.Fori(0, T) as t:
                    x_from, h_from = row_sources(l, t)
                    sp.dma_start(d_adj, rows_of(adj, t)).then_inc(d_in, 16)
                    sp.dma_start(row[:, 0, 0:F], x_from).then_inc(d_in, 16)
                    sp.dma_start(row[:, 0, F:XW], h_from).then_inc(d_in, 16)
                    with sp.Fori(0, T) as c:
                        sp.dma_start(d_h, rows_of(table[l][:, 0:F], c, 1)).then_inc(d_h_in, 16)
                        sp.wait_ge(d_mm_done, (T * l + t) * T + c + 1)
                        sp.sem_inc(passed, 1)
                    sp.wait_ge(mv_done, T * (l + 1) + t + 1)
                    sp.sem_inc(passed, 1)
            sp.wait_ge(d_kept_out, 16 * T * 3)
            sp.wait_ge(d_tab_out, 16 * T * 3)
            with sp.Fori(0, T) as c:
                sp.dma_start(d_h, rows_of(table[3][:, 0:F], c, 1)).then_inc(d_h_in, 16)
                sp.wait_ge(d_partT_done, 3 * T * T + c + 1)
                sp.sem_inc(passed, 1)
            with sp.Fori(0, N) as i:
                sp.dma_start(d_adj, adj[bass.ds(i, 1), :].broadcast_to([P, N])).then_inc(d_row_in, 16)
                sp.wait_ge(d_col_done, i + 1)
                sp.sem_inc(passed, 1)
            with sp.Fori(0, T) as t:
                sp.dma_start(row[:, 0, 0:F], rows_of(kept[3][:, 0:F], t)).then_inc(d_in, 16)
                sp.wait_ge(x_new, 3 * T + t + 1)
                sp.sem_inc(passed, 1)
                sp.dma_start(rows_of(out, t), new[:, 0, 0:F]).then_inc(d_out, 16)
                sp.wait_ge(d_out, 16 * (t + 1))
                sp.sem_inc(passed, 1)

        def dense_pe(pe):
            for l in range(3):
                with pe.Fori(0, T) as t:
                    with pe.Fori(0, T) as c:
                        q = (T * l + t) * T + c
                        pe.wait_ge(d_part_done, q + 1)
                        nc.tensor.transpose(hT_ps[0], d_part, ident[:]).then_inc(d_partT_done, 1)
                        pe.wait_ge(d_turn_done, q + 1)
                        pe.wait_ge(d_h_in, 16 * (q + 1))
                        nc.tensor.matmul(hw_ps[0][:, 0:F], hnT[:, 0, :], d_h, start=True, stop=True).then_inc(d_mm_done, 1)
                    node_pe(pe, 0, T * (l + 1) + t, l + 1)
            with pe.Fori(0, T) as c:
                pe.wait_ge(d_h_in, 16 * (3 * T * T + c + 1))
                pe.wait_ge(hn_done, 4 * T)
                nc.tensor.transpose(hT_ps[0], d_h, ident[:]).then_inc(d_partT_done, 1)
                pe.wait_ge(d_turn_done, 3 * T * T + c + 1)
                pe.sem_inc(passed, 1)
            with pe.Fori(0, T) as t:
                pe.wait_ge(d_part_done, 3 * T * T + t + 1)
                nc.tensor.transpose(hT_ps[0], d_part, ident[:]).then_inc(d_partT_done, 1)

        def dense_act(act):
            act.wait_ge(dummy_out, 16 * LAYERS)
            act.wait_ge(recx_in, 16 * T)
            for l in range(3):
                with act.Fori(0, T) as t:
                    g = T * l + t
                    m = T + g
                    act.wait_ge(nemax_done, g + 1)
                    nc.scalar.activation(d_score, d_score, ACT.Exp, bias=nemax[:, 0:1],
                                         accum_out=psum_p[:, 0:1]).then_inc(prob_done, 1)
                    with act.Fori(0, T) as c:
                        act.wait_ge(d_partT_done, g * T + c + 1)
                        nc.scalar.activation(hnT[:, 0, :], hT_ps[0], ACT.Copy).then_inc(d_turn_done, 1)
                    if l < 2:
                        act.wait_ge(zneg_done, g + 1)
                        nc.scalar.activation(ez[:, 0, :], zneg[:, 0, :], ACT.Exp).then_inc(ez_done, 1)
                    node_act_std(act, 0, m)
                    node_act(act, 0, m, l + 1, lambda: None)
                    if l == 0:
                        act.wait_ge(tflag_done, t + 1)
                    if l == 1:
                        act.wait_ge(row_done, rows_after(2, t))
                    if l == 2:
                        act.wait_ge(hn_done, m + 1)
                    act.dma_start(rows_of(kept[l + 1], t), new[:, 0, :]).then_inc(d_kept_out, 16)
                    act.dma_start(rows_of(table[l + 1], t, 1), new[:, 0, F:XW]).then_inc(d_tab_out, 16)
                    act.wait_ge(d_kept_out, 16 * (g + 1))
                    act.wait_ge(d_tab_out, 16 * (g + 1))
                    act.sem_inc(passed, 1)
            with act.Fori(0, T) as c:
                act.wait_ge(d_partT_done, 3 * T * T + c + 1)
                act.sem_inc(passed, 1)
                nc.scalar.activation(d_score[:, bass.ds(c * P, P)], hT_ps[0], ACT.Copy).then_inc(d_turn_done, 1)

        def dense_dve(dve):
            for l in range(3):
                dve.wait_ge(d_t_in, 48 * (l + 1))
                with dve.Fori(0, T) as t:
                    g = T * l + t
                    m = T + g
                    big = (NEG0, NEG1, NEG1)[l]
                    dve.wait_ge(d_in, 48 * (g + 1))
                    nc.vector.tensor_scalar(d_mask, d_adj, 0.0, None, ALU.is_gt).then_inc(d_mask_done, 1)
                    dve.wait_ge(d_mask_done, g + 1)
                    if l == 1:
                        nc.vector.tensor_scalar(d_score, d_t, FAR / 10, None, ALU.is_gt).then_inc(ok_done, 1)
                        dve.wait_ge(ok_done, t + 1)
                        nc.vector.tensor_tensor(d_mask, d_mask, d_score, ALU.mult).then_inc(d_ok_done, 1)
                        dve.wait_ge(d_ok_done, t + 1)
                        nc.vector.tensor_reduce(count[:], d_mask, AX_X, ALU.add).then_inc(d_cnt_done, 1)
                    nc.vector.tensor_scalar(d_neg, d_mask, big, -big, ALU.mult, ALU.add).then_inc(d_neg_done, 1)
                    nc.vector.tensor_scalar(d_score, d_t, row[:, 0, X_S:X_S + 1], None, ALU.add).then_inc(e1_done, 1)
                    dve.wait_ge(e1_done, g + 1)
                    nc.vector.scalar_tensor_tensor(out=d_score, in0=d_score, scalar=SLOPE, in1=d_score,
                                                   op0=ALU.mult, op1=ALU.max).then_inc(e2_done, 1)
                    dve.wait_ge(e2_done, g + 1)
                    if l < 2:
                        nc.vector.tensor_tensor(d_score, d_score, d_mask, ALU.mult).then_inc(gw_done, 1)
                        dve.wait_ge(gw_done, g + 1)
                    dve.wait_ge(d_neg_done, g + 1)
                    nc.vector.tensor_tensor(d_score, d_score, d_neg, ALU.add).then_inc(d_add_done, 1)
                    dve.wait_ge(d_add_done, g + 1)
                    nc.vector.tensor_reduce(emax[:], d_score, AX_X, ALU.max).then_inc(emax_done, 1)
                    dve.wait_ge(emax_done, g + 1)
                    nc.vector.tensor_scalar(nemax[:, 0:1], emax[:], -1.0, None, ALU.mult).then_inc(nemax_done, 1)
                    nc.vector.memset(agg[:], 0.0).then_inc(d_clear_done, 1)
                    dve.wait_ge(prob_done, g + 1)
                    nc.vector.reciprocal(rsum[:], psum_p[:, 0:1]).then_inc(rsum_done, 1)
                    dve.wait_ge(rsum_done, g + 1)
                    factor = rsum
                    if l == 1:
                        nc.vector.scalar_tensor_tensor(out=d_score, in0=d_score, scalar=rsum[:], in1=d_mask,
                                                       op0=ALU.mult, op1=ALU.mult).then_inc(share_done, 1)
                        dve.wait_ge(share_done, t + 1)
                        nc.vector.tensor_reduce(top[:], d_score, AX_X, ALU.max).then_inc(top_done, 1)
                        dve.wait_ge(top_done, t + 1)
                        nc.vector.scalar_tensor_tensor(out=d_score, in0=d_score, scalar=THR, in1=d_score,
                                                       op0=ALU.is_ge, op1=ALU.mult).then_inc(wgt_done, 1)
                        dve.wait_ge(d_cnt_done, t + 1)
                        nc.vector.tensor_scalar(fac[:], top[:], THR, count[:], ALU.is_gt, ALU.mult).then_inc(fac_done, 1)
                        dve.wait_ge(wgt_done, t + 1)
                        dve.wait_ge(fac_done, t + 1)
                        factor = fac
                    dve.wait_ge(d_clear_done, g + 1)
                    dve.sem_inc(passed, 1)
                    with dve.Fori(0, T) as c:
                        q = g * T + c
                        nc.vector.tensor_copy(d_part, d_score[:, bass.ds(c * P, P)]).then_inc(d_part_done, 1)
                        dve.wait_ge(d_mm_done, q + 1)
                        nc.vector.tensor_tensor(agg[:], agg[:], hw_ps[0][:, 0:F], ALU.add).then_inc(d_acc_done, 1)
                        dve.wait_ge(d_acc_done, q + 1)
                        dve.sem_inc(passed, 1)
                    x_row = row[:, 0, 0:F]
                    if l == 2:
                        nc.vector.scalar_tensor_tensor(out=new[:, 0, 0:F], in0=agg[:], scalar=factor[:], in1=x_row,
                                                       op0=ALU.mult, op1=ALU.add).then_inc(x_new, 1)
                    else:
                        elu_residual(dve, g, 0, l, factor, x_row, agg[:])
                    dve.wait_ge(x_new, g + 1)
                    node_dve_stats(dve, 0, m, new[:, 0, 0:F])
                    node_dve_norm(dve, 0, m, new[:, 0, 0:F])
                    if l == 0:
                        mark_unattendable(dve, 0, t)
                    dve.wait_ge(d_kept_out, 16 * (g + 1))
                    dve.wait_ge(d_tab_out, 16 * (g + 1))
                    dve.sem_inc(passed, 1)
            dve.wait_ge(d_turn_done, 3 * T * T + T)
            with dve.Fori(0, N) as i:
                dve.wait_ge(d_row_in, 16 * (i + 1))
                nc.vector.tensor_scalar(d_mask, d_adj, 0.0, None, ALU.not_equal).then_inc(d_rmask_done, 1)
                dve.wait_ge(d_rmask_done, i + 1)
                nc.vector.tensor_tensor(d_neg, d_score, d_mask, ALU.mult).then_inc(d_prod_done, 1)
                dve.wait_ge(d_prod_done, i + 1)
                nc.vector.tensor_reduce(emax[:], d_neg, AX_X, ALU.max).then_inc(d_max_done, 1)
                dve.wait_ge(d_max_done, i + 1)
                nc.vector.tensor_scalar(d_t[:, bass.ds(i, 1)], emax[:], 1.0, None, ALU.mult).then_inc(d_col_done, 1)
            dve.wait_ge(d_col_done, N)
            with dve.Fori(0, T) as t:
                q = 3 * T * T + t
                nc.vector.tensor_copy(d_part, d_t[:, bass.ds(t * P, P)]).then_inc(d_part_done, 1)
                dve.wait_ge(d_partT_done, q + T + 1)
                dve.wait_ge(d_in, 48 * 3 * T + 16 * (t + 1))
                nc.vector.tensor_tensor(new[:, 0, 0:F], hT_ps[0], row[:, 0, 0:F], ALU.add).then_inc(x_new, 1)
                dve.wait_ge(d_out, 16 * (t + 1))
                dve.sem_inc(passed, 1)

        def elu_residual(dve, g, b, l, factor, x_row, sums_):
            if l == 0:
                nc.vector.tensor_scalar(z[:, b, :], sums_, factor[:], None, ALU.mult).then_inc(z_done, 1)
            else:
                nc.vector.scalar_tensor_tensor(out=z[:, b, :], in0=sums_, scalar=factor[:], in1=row[:, b, F:2 * F],
                                               op0=ALU.mult, op1=ALU.add).then_inc(z_done, 1)
            dve.wait_ge(z_done, g + 1)
            nc.vector.tensor_scalar(zneg[:, b, :], z[:, b, :], 0.0, None, ALU.min).then_inc(zneg_done, 1)
            dve.wait_ge(ez_done, g + 1)
            nc.vector.scalar_tensor_tensor(out=z1, in0=z[:, b, :], scalar=0.0, in1=ez[:, b, :],
                                           op0=ALU.max, op1=ALU.add).then_inc(z1_done, 1)
            dve.wait_ge(z1_done, g + 1)
            nc.vector.scalar_tensor_tensor(out=new[:, b, 0:F], in0=z1, scalar=-1.0, in1=x_row,
                                           op0=ALU.add, op1=ALU.add).then_inc(x_new, 1)

        def mark_unattendable(dve, b, t):
            dve.wait_ge(row_done, rows_after(1, t))
            nc.vector.tensor_scalar(hzero[:], hsum[:, b:b + 1], 0.0, FAR, ALU.is_equal, ALU.mult).then_inc(hzero_done, 1)
            dve.wait_ge(hzero_done, t + 1)
            nc.vector.tensor_tensor(new[:, b, X_T:X_T + 1], new[:, b, X_T:X_T + 1], hzero[:],
                                    ALU.add).then_inc(tflag_done, 1)

        @block.sync
        def _(sp):
            sp.dma_start(w_sb[0][:], w0).then_inc(w_in, 16)
            sp.dma_start(w_sb[1][:], w1).then_inc(w_in, 16)
            for l, a in enumerate((a0, a1, a2)):
                sp.dma_start(att[l][:, 0:1], a[F:2 * F, :]).then_inc(w_in, 16)
                sp.dma_start(att[l][:, 1:2], a[0:F, :]).then_inc(w_in, 16)

            def load_adj(t, b):
                sp.dma_start(adj_t[:, b, :], rows_of(adj, t)).then_inc(adj_in[b], 16)

            def load_x(t, b):
                sp.dma_start(new[:, b, 0:F], rows_of(x, t)).then_inc(x_in[b], 16)
                sp.dma_start(rec[:, t, R_X:R_X + F], rows_of(x, t)).then_inc(recx_in, 16)

            load_adj(0, 0)
            load_x(0, 0)
            load_adj(1, 1)
            for first, last in ((0, 1), (1, PAIRS - 1)):
                for i in pairs_of(sp, first, last) if last > first else ():
                    for b in range(2):
                        t = 2 * i + b
                        sp.wait_ge(plain_done, t + 1)
                        sp.sem_inc(passed, 1)
                        load_adj(t + 2, b)
                        at_least(sp, xn_done, t)
                        sp.sem_inc(passed, 1)
                        load_x(t + 1, 1 - b)
            sp.wait_ge(xn_done, T - 2)
            load_x(T - 1, 1)
            sp.wait_ge(verdict_done, 1)
            v = sp.value_load(verdict[0:1, 0:1], min_val=0, max_val=2 ** 30)
            with sp.If(v < 1):
                def load_h(l):
                    sp.dma_start(w_h, table[l][1:N + 1, :].rearrange("(c p) w -> p c w", p=P)).then_inc(w_h_in, 16)

                def store_t(l):
                    sp.wait_ge(w_tT_sb, l + 1)
                    sp.dma_start(t_all[l], w_tT[:]).then_inc(w_t_out, 16)
                    sp.wait_ge(w_min_done, l + 1)
                    sp.dma_start(t_min[l], w_tile_min).then_inc(w_t_out, 16)
                    sp.wait_ge(w_t_out, 32 * (l + 1))

                def spread_t(l):
                    if l:
                        sp.wait_ge(w_u_done, ND * l)
                        sp.wait_ge(w_max_done, ND * l)
                    sp.dma_start(w_mins[:], t_min[l].rearrange("t one -> one t").broadcast_to([P, T])).then_inc(w_t_in, 16)
                    sp.dma_start(w_t, t_all[l].rearrange("t p -> (t p)")[None, :].broadcast_to([P, N])).then_inc(w_t_in, 16)

                def load_idx(x_):
                    sp.dma_start(idx[x_.b][:], rows_of(srt.bitcast(U32)[:, 0:R_X], x_.t)).then_inc(idx_in[x_.b], 16)

                def load_row(x_):
                    b = x_.b
                    if x_.l:
                        sp.dma_start(row[:, b, :], rows_of(kept[x_.l], x_.t)).then_inc(row_in[b], 16)
                    else:
                        sp.dma_start(row[:, b, 0:2 * F + 2], rows_of(srt[:, R_X:RW], x_.t)).then_inc(row_in[b], 16)

                def load_s(x_):
                    if x_.l:
                        sp.dma_start(w_s[:], rows_of(kept[x_.l][:, X_T:X_T + 2], x_.t)).then_inc(w_s_in, 16)
                    else:
                        sp.dma_start(w_s[:], rows_of(srt[:, RW - 2:RW], x_.t)).then_inc(w_s_in, 16)

                def load_behind(done, following):
                    sp.wait_ge(g_in[done.b], 16 * done.gathered)
                    sp.sem_inc(passed, 1)
                    sp.wait_ge(rid_done[done.b], done.used + 1)
                    sp.sem_inc(passed, 1)
                    load_idx(following)
                    sp.wait_ge(x_new, done.g + 1)
                    sp.sem_inc(passed, 1)
                    load_row(following)

                for l in range(3):
                    if l:
                        for b in range(3):
                            sp.wait_ge(kept_out[b], 16 * uses(l, b))
                            sp.wait_ge(tab_out[b], 16 * uses(l, b))
                        sp.wait_ge(rid_done[0], uses(l, 0))
                        sp.wait_ge(rid_done[1], uses(l, 1))
                        sp.wait_ge(rid_done[WIDE], uses(l, WIDE))
                        sp.wait_ge(w_cols, uses(l, WIDE))
                        sp.wait_ge(x_new, T * l)
                        sp.wait_ge(w_multiplied, NDG * l)
                    else:
                        for b in range(2):
                            sp.wait_ge(tab_nat[b], 16 * PAIRS)
                    if l == 0:
                        load_h(l)
                        store_t(l)
                        sp.wait_ge(sorted_out, 16 * T)
                    for j in range(2):
                        x_ = gathered_tile(l, 0, 0, turn_caps[0], j)
                        load_idx(x_)
                        load_row(x_)
                    load_idx(wide_tile(l, 0))
                    load_row(wide_tile(l, 0))
                    load_s(wide_tile(l, 0))
                    if l:
                        load_h(l)
                        store_t(l)
                    spread_t(l)
                    for first, last, caps in turns:
                        for k in pairs_of(sp, first, last):
                            some = [gathered_tile(l, k, first, caps, j) for j in range(len(caps))]
                            wide = wide_tile(l, k)
                            for j, x_ in enumerate(some):
                                if j + 2 < len(some):
                                    load_behind(x_, some[j + 2])
                                elif last < TURNS:
                                    load_behind(x_, gathered_tile(l, k + 1, last, turn_caps[last], j + 2 - len(some)))
                                if j == 1 and first and last < TURNS:
                                    sp.wait_ge(x_new, wide_tile(l, k - 1).g + 1)
                                    sp.sem_inc(passed, 1)
                                    load_row(wide)
                                if j == 2 and last < TURNS - 1:
                                    sp.wait_ge(w_cols, wide.used + 1)
                                    sp.sem_inc(passed, 1)
                                    load_s(wide_tile(l, k + 1))
                                if j == 4 and last < TURNS - 1:
                                    sp.wait_ge(w_adj_in, 16 * (wide.used + 1))
                                    sp.wait_ge(rid_done[WIDE], wide.used + 1)
                                    sp.sem_inc(passed, 1)
                                    load_idx(wide_tile(l, k + 1))
                for b in range(3):
                    sp.wait_ge(kept_out[b], 16 * uses(3, b))
                    sp.wait_ge(rid_done[b], uses(3, b))
                sp.wait_ge(x_new, T * 3)
                for b in range(2):
                    x_ = last_layer_tile(0, 0, pair_caps[0], b)
                    load_idx(x_)
                    load_row(x_)
                for first, last, cap in groups:
                    for i in pairs_of(sp, first, min(last, PAIRS - 1)) if first < PAIRS - 1 else ():
                        for b in range(2):
                            load_behind(last_layer_tile(i, first, cap, b), last_layer_tile(i + 1, first, cap, b))
            with sp.Else():
                dense_loads(sp)

        @block.gpsimd
        def _(pool):
            nc.gpsimd.iota(pos[:], [[1, BLK]], base=1, channel_multiplier=0,
                           allow_small_or_imprecise_dtypes=True).then_inc(const_pool, 1)
            nc.gpsimd.iota(blk_base[:], [[BLK, NBLK], [0, TOP]], base=0, channel_multiplier=0,
                           allow_small_or_imprecise_dtypes=True).then_inc(const_pool, 1)
            nc.gpsimd.iota(cls[:], [[-1, C]], base=DMAX, channel_multiplier=0,
                           allow_small_or_imprecise_dtypes=True).then_inc(const_pool, 1)
            nc.gpsimd.iota(node[:, :, 0], [[P, T]], base=1, channel_multiplier=1).then_inc(const_pool, 1)
            nc.gpsimd.iota(node[:, :, 1], [[P, T]], base=0, channel_multiplier=1).then_inc(const_pool, 1)
            nc.gpsimd.iota(node_f[:], [[P, T]], base=1, channel_multiplier=1,
                           allow_small_or_imprecise_dtypes=True).then_inc(const_pool, 1)
            nc.gpsimd.memset(ones_f[:], 1.0).then_inc(const_pool, 1)
            nc.gpsimd.memset(ones_b[:], 1.0).then_inc(const_pool, 1)
            nc.gpsimd.memset(eps[:], EPS).then_inc(const_pool, 1)
            pool.wait_ge(const_pool, 9)
            nc.gpsimd.affine_select(out=ident[:], in_=ones_f[:], compare_op=ALU.is_equal, fill=0.0, base=0,
                                    pattern=[[-1, P]], channel_multiplier=1).then_inc(const_pool, 1)
            nc.gpsimd.affine_select(out=tri[:], in_=ones_b[:], compare_op=ALU.is_gt, fill=0.0, base=0,
                                    pattern=[[1, P]], channel_multiplier=-1).then_inc(const_pool, 1)
            with pool.Fori(0, PAIRS) as i:
                for b in range(2):
                    pool.wait_ge(sq_done, 2 * i + b + 1)
                    part = sq[b][:, 0:POOL_BLK * BLK].rearrange("p (n w) -> p n w", w=BLK)
                    nc.gpsimd.tensor_tensor(part, part, pos[:, None, :].broadcast_to([P, POOL_BLK, BLK]),
                                            ALU.mult).then_inc(key_pool, 1)
            pool.wait_ge(verdict_done, 1)
            v = pool.value_load(verdict[0:1, 0:1], min_val=0, max_val=2 ** 30)
            with pool.If(v < 1):
                pool.wait_ge(recx_in, 16 * T)
                pool.wait_ge(s_kept, 2 * T)
                for t in range(T):
                    nc.gpsimd.indirect_dma_start(srt, bass.IndirectOffsetOnAxis(rank_u[:, t:t + 1], 0),
                                                 rec[:, t, :], None).then_inc(sorted_out, 16)
                for b in range(2):
                    pool.wait_ge(tab_nat[b], 16 * PAIRS)
                pool.wait_ge(dummy_out, 16 * LAYERS)

                def scatter(x_):
                    l, b = x_.l, x_.b
                    if l == 0:
                        pool.wait_ge(tflag_done, x_.n + 1)
                    elif l == 1:
                        pool.wait_ge(row_done, rows_after(2, x_.n))
                    elif l == 2:
                        pool.wait_ge(hn_done, x_.m + 1)
                    else:
                        pool.wait_ge(rid_done[b], x_.used + 1)
                        pool.wait_ge(x_new, x_.g + 1)
                    pool.sem_inc(passed, 1)
                    if l < 3:
                        nc.gpsimd.indirect_dma_start(table[l + 1], bass.IndirectOffsetOnAxis(rid[b][:, 0:1], 0),
                                                     new[:, b, F:XW], None).then_inc(tab_out[b], 16)
                    else:
                        nc.gpsimd.indirect_dma_start(out, bass.IndirectOffsetOnAxis(rid[b][:, 1:2], 0),
                                                     new[:, b, 0:F], None).then_inc(res_out[b], 16)

                def gather(x_):
                    l, b, cap = x_.l, x_.b, x_.cap
                    pool.wait_ge(idx_in[b], 16 * (x_.used + 1))
                    at_least(pool, agg_done[b], x_.used)
                    pool.sem_inc(passed, 1)
                    for k in range(cap):
                        nc.gpsimd.indirect_dma_start(
                            gath[b][:, k, :], None, table[l],
                            bass.IndirectOffsetOnAxis(idx[b][:, k:k + 1], 0)).then_inc(g_in[b], 16)

                for l in range(3):
                    if l:
                        for b in range(3):
                            pool.wait_ge(tab_out[b], 16 * uses(l, b))
                    for first, last, caps in turns:
                        for k in pairs_of(pool, first, last):
                            some = [gathered_tile(l, k, first, caps, j) for j in range(len(caps))]
                            for j, x_ in enumerate(some):
                                gather(x_)
                                if j == 3 and first:
                                    scatter(wide_tile(l, k - 1))
                                if j > 1:
                                    scatter(some[j - 2])
                                elif first:
                                    before = turn_caps[first - 1]
                                    scatter(gathered_tile(l, k - 1, first - 1, before, len(before) - 2 + j))
                                if j == 0 and last < TURNS:
                                    x_ = wide_tile(l, k)
                                    if l == 0 and first == 0:
                                        pool.wait_ge(sorted_out, 16 * T)
                                    pool.wait_ge(idx_in[WIDE], 16 * (x_.used + 1))
                                    at_least(pool, w_p_done, x_.used)
                                    if l:
                                        at_least(pool, w_cnt_done, x_.used - ND if l == 1 else ND)
                                    pool.sem_inc(passed, 1)
                                    nc.gpsimd.indirect_dma_start(
                                        w_adj.bitcast(I32), None, adj,
                                        bass.IndirectOffsetOnAxis(idx[WIDE][:, R_OUT:R_OUT + 1], 0)).then_inc(w_adj_in, 16)
                    for j in (2, 1):
                        scatter(gathered_tile(l, TURNS - 1, TURNS - 1, turn_caps[-1], len(turn_caps[-1]) - j))
                for b in range(3):
                    pool.wait_ge(tab_out[b], 16 * uses(3, b))
                for first, last, cap in groups:
                    for i in pairs_of(pool, first, last):
                        for b in range(2):
                            gather(last_layer_tile(i, first, cap, b))
                            if b:
                                scatter(last_layer_tile(i, first, cap, 0))
                            elif first:
                                scatter(last_layer_tile(i - 1, first, cap, 1))
                scatter(last_layer_tile(PAIRS - 1, 0, pair_caps[-1], 1))
                for b in range(2):
                    pool.wait_ge(res_out[b], 16 * PAIRS)

        @block.scalar
        def _(act):
            for l in range(2):
                act.wait_ge(wT_ps, l + 1)
                nc.scalar.activation(wT[l], hT_ps[l], ACT.Copy).then_inc(wT_sb, 1)
            for l in range(2):
                act.wait_ge(wa_ps, l + 1)
                nc.scalar.activation(wx[l][:, 0:F], w_sb[l][:], ACT.Copy).then_inc(wx_done, 1)
                nc.scalar.activation(wx[l][:, F:F + 2], hw_ps[l][:, 0:2], ACT.Copy).then_inc(wx_done, 1)
            act.wait_ge(dummy_set, 2)
            act.wait_ge(const_dve, 1)
            for l in range(LAYERS):
                act.dma_start(table[l][0:1, :], no_row[:]).then_inc(dummy_out, 16)
            act.wait_ge(const_pool, 11)

            def square(t, b):
                nc.scalar.activation(sq[b][:], adj_t[:, b, :], ACT.Square,
                                     accum_out=squares[:, bass.ds(t, 1)]).then_inc(sq_done, 1)

            def sum_plain(t, b):
                act.wait_ge(sq_done, t + 1)
                nc.scalar.activation(adj_t[:, b, :], adj_t[:, b, :], ACT.Copy,
                                     accum_out=plain[:, bass.ds(t, 1)]).then_inc(plain_done, 1)

            def keep_list(t, b):
                act.wait_ge(deg_done, t + 1)
                act.sem_inc(passed, 1)
                nc.scalar.activation(rec[:, t, 0:KMAX].bitcast(U32), lst[:, b, :], ACT.Copy).then_inc(lst_free, 1)
                nc.scalar.activation(rec[:, t, R_TAB:R_X].bitcast(U32), node[:, t, :], ACT.Copy).then_inc(s_kept, 1)

            def rows(i, b):
                t = 2 * i + b

                def table_row_left():
                    at_least(act, tab_nat[b], 16 * i)
                node_act(act, b, t, 0, table_row_left)
                act.wait_ge(row_done, 2 * (t + 1))
                act.dma_start(rows_of(table[0], t, 1), new[:, b, F:XW]).then_inc(tab_nat[b], 16)
                act.sem_inc(passed, 1)
                nc.scalar.activation(rec[:, t, R_X + F:RW], new[:, b, F:2 * F + 2], ACT.Copy).then_inc(s_kept, 1)

            def natural(i, b):
                t = 2 * i + b
                if not (isinstance(t, int) and t == T - 1):
                    act.wait_ge(adj_in[1 - b], 16 * (i + 1 + b))
                    at_least(act, max_done, t)
                    act.sem_inc(passed, 1)
                    square(t + 1, 1 - b)
                node_act_std(act, b, t)
                if not (isinstance(t, int) and t == 0):
                    rows(i - 1 + b, 1 - b)
                if b == 0 and not (isinstance(i, int) and i == 0):
                    for c in range(2):
                        keep_list(2 * (i - 1) + c, c)
                if not (isinstance(t, int) and t == T - 1):
                    sum_plain(t + 1, 1 - b)

            act.wait_ge(adj_in[0], 16)
            square(0, 0)
            sum_plain(0, 0)
            for first, last in ((0, 1), (1, PAIRS - 1), (PAIRS - 1, PAIRS)):
                for i in pairs_of(act, first, last) if last > first else ():
                    for b in range(2):
                        natural(i, b)
            rows(PAIRS - 1, 1)
            for c in range(2):
                keep_list(T - 2 + c, c)
            act.wait_ge(verdict_done, 1)
            v = act.value_load(verdict[0:1, 0:1], min_val=0, max_val=2 ** 30)
            with act.If(v < 1):

                def copy_row_numbers(x_):
                    b = x_.b
                    act.wait_ge(idx_in[b], 16 * (x_.used + 1))
                    at_least(act, tab_out[b], 16 * (x_.used if x_.l < 3 else uses(3, b)))
                    if x_.l == 3:
                        at_least(act, res_out[b], 16 * x_.u)
                    nc.scalar.activation(rid[b][:], idx[b][:, R_TAB:R_X], ACT.Copy).then_inc(rid_done[b], 1)

                def finish(x_):
                    l, b = x_.l, x_.b
                    if l < 2:
                        act.wait_ge(zneg_done, x_.g + 1)
                        nc.scalar.activation(ez[:, b, :], zneg[:, b, :], ACT.Exp).then_inc(ez_done, 1)

                    def kept_left():
                        at_least(act, kept_out[b], 16 * x_.used)
                    node_act_std(act, b, x_.m)
                    node_act(act, b, x_.m, l + 1, kept_left)
                    if l == 0:
                        act.wait_ge(tflag_done, x_.n + 1)
                    if l == 1:
                        act.wait_ge(row_done, rows_after(2, x_.n))
                    if l == 2:
                        act.wait_ge(hn_done, x_.m + 1)
                    act.dma_start(rows_of(kept[l + 1], x_.t), new[:, b, :]).then_inc(kept_out[b], 16)

                def gathered(x_, meanwhile=lambda: None):
                    l, b, cap = x_.l, x_.b, x_.cap
                    act.wait_ge(row_in[b], 16 * (x_.used + 1))
                    at_least(act, agg_done[b], x_.used)
                    nc.scalar.activation(gath[b][:, cap, 0:F + 2], row[:, b, F:2 * F + 2], ACT.Copy).then_inc(own_done, 1)
                    if l < 3:
                        act.wait_ge(nemax_done, x_.s + 1)
                        kw = {} if l == 1 else {"accum_out": psum_p[:, b:b + 1]}
                        nc.scalar.activation(prob[:, b, 0:cap + 1], e2[:, b, 0:cap + 1], ACT.Exp,
                                             bias=nemax[:, b:b + 1], **kw).then_inc(prob_done, 1)
                    copy_row_numbers(x_)
                    meanwhile()
                    if l < 3:
                        finish(x_)

                def copy_turned(x_, quads):
                    for c in quads:
                        q = NQ * x_.used + c
                        act.wait_ge(w_turned, q + 1)
                        at_least(act, w_multiplied, q - 1)
                        nc.scalar.activation(w_eT[:, c % 2, :], eT_ps[:, c % 2, :], ACT.Copy).then_inc(w_copied, 1)

                for l in range(3):
                    act.wait_ge(w_tT_ps, l + 1)
                    nc.scalar.activation(w_tT[:], banks[0:T, 7, 0:P], ACT.Copy).then_inc(w_tT_sb, 1)
                    for first, last, caps in turns:
                        for k in pairs_of(act, first, last):
                            some = [gathered_tile(l, k, first, caps, j) for j in range(len(caps))]
                            wide, done = wide_tile(l, k), wide_tile(l, k - 1)

                            def wide_step():
                                if j < 2 and first:
                                    copy_turned(done, QUADS[j])
                                if last == TURNS:
                                    return
                                if j == 2:
                                    at_least(act, w_turned, NQ * wide.used)
                                    act.wait_ge(w_cols, wide.used + 1)
                                    nc.scalar.activation(w_e, w_t, ACT.Identity, bias=w_us[:]).then_inc(w_u_done, 1)
                                if j == 3:
                                    act.wait_ge(w_lrelu_done, wide.used + 1)
                                    act.wait_ge(w_m_done, wide.used + 1)
                                    nc.scalar.activation(w_e, w_e, ACT.Exp, bias=w_negm[:]).then_inc(w_exp_done, 1)
                                if j == 4 and l == 1:
                                    act.wait_ge(w_max_done, wide.used + 1)
                                    at_least(act, w_fac_done, wide.used - ND)
                                    nc.scalar.activation(w_adj, w_adj, ACT.Sign, accum_out=w_cnt[:]).then_inc(w_cnt_done, 1)
                                if j == 5:
                                    copy_turned(wide, QUADS[j])

                            for j, x_ in enumerate(some):
                                gathered(x_, wide_step)
                                if j == 1 and first:
                                    finish(done)
                                if j == 4 and last < TURNS:
                                    copy_row_numbers(wide)
                for first, last, cap in groups:
                    for i in pairs_of(act, first, last):
                        for b in range(2):
                            x_ = last_layer_tile(i, first, cap, b)
                            gathered(x_)
                for b in range(3):
                    act.wait_ge(kept_out[b], 16 * uses(3, b))
            with act.Else():
                dense_act(act)

        @block.tensor
        def _(pe):
            pe.wait_ge(w_in, 16 * 8)
            pe.wait_ge(const_pool, 11)
            for l in range(2):
                nc.tensor.transpose(hT_ps[l], w_sb[l][:], ident[:]).then_inc(wT_ps, 1)
            for l in range(2):
                pe.wait_ge(wT_sb, l + 1)
                nc.tensor.matmul(hw_ps[l][:, 0:2], wT[l], att[l][:], start=True, stop=True).then_inc(wa_ps, 1)
            pe.wait_ge(wx_done, 4)
            with pe.Fori(0, PAIRS) as i:
                for b in range(2):
                    node_pe(pe, b, 2 * i + b, 0)
            pe.wait_ge(dv, 1)
            pe.wait_ge(row_done, 2 * T)
            for c0, c1 in CT_CHUNKS:
                last = nc.tensor.matmul(rank_ps[:, c0:c1], ones_b[:], eq[:, c0:c1], start=True, stop=True)
            last.then_inc(tot_ps, 1)
            pe.wait_ge(tot_sb, 1)
            for c0, c1 in CT_CHUNKS:
                last = nc.tensor.matmul(rank_ps[:, c0:c1], tri[:], eq[:, c0:c1], start=True, stop=True)
            last.then_inc(tri_ps, 1)
            pe.wait_ge(bad_ps, 1)
            nc.tensor.matmul(hw_ps[0][:, 0:1], ones_f[:], bad_sum[:], start=True, stop=True).then_inc(bad_ps, 1)
            pe.wait_ge(verdict_done, 1)
            v = pe.value_load(verdict[0:1, 0:1], min_val=0, max_val=2 ** 30)
            with pe.If(v < 1):
                def turn_and_multiply(x_, quads):
                    for c in quads:
                        q = NQ * x_.used + c
                        at_least(pe, w_copied, q - 1)
                        for j in range(4):
                            at = (4 * c + j) * P
                            last_ = nc.tensor.transpose(eT_ps[:, c % 2, j * P:(j + 1) * P], w_e[:, at:at + P], ident[:])
                        last_.then_inc(w_turned, 1)
                        if c:
                            multiply(x_, c - 1)

                def multiply(x_, c):
                    q = NQ * x_.used + c
                    pe.wait_ge(w_copied, q + 1)
                    for j in range(4):
                        last_ = nc.tensor.matmul(acc_ps, w_eT[:, c % 2, j * P:(j + 1) * P], w_h[:, 4 * c + j, 0:F],
                                                 start=(c == 0 and j == 0), stop=(c == NQ - 1 and j == 3))
                    last_.then_inc(w_multiplied, 1)

                for l in range(3):
                    pe.wait_ge(w_h_in, 16 * (l + 1))
                    at_least(pe, hw_done, T * (l + 1))
                    if l:
                        pe.wait_ge(row_done, rows_after(l, T - 1))
                    nc.tensor.transpose(banks[0:T, 7, 0:P], w_h[:, :, F], ident[:]).then_inc(w_tT_ps, 1)
                    for first, last, caps in turns:
                        for k in pairs_of(pe, first, last):
                            wide, done = wide_tile(l, k), wide_tile(l, k - 1)
                            for j in range(len(caps)):
                                if j < 2 and first:
                                    turn_and_multiply(done, QUADS[j])
                                if j == 1 and first:
                                    multiply(done, NQ - 1)
                                if j == 5 and last < TURNS:
                                    pe.wait_ge(*scores_ready(wide))
                                    at_least(pe, x_new, T * l + (7 * k + 2 if first else 0))
                                    turn_and_multiply(wide, QUADS[j])
                                node_pe(pe, j % 2, gathered_tile(l, k, first, caps, j).m, l + 1)
                                if j == 1 and first:
                                    node_pe(pe, WIDE, done.m, l + 1)
            with pe.Else():
                dense_pe(pe)

        @block.vector
        def _(dve):
            nc.vector.memset(no_row[:], 0.0).then_inc(dummy_set, 1)
            dve.wait_ge(dummy_set, 1)
            nc.vector.memset(no_row[:, F:F + 1], FAR).then_inc(dummy_set, 1)
            nc.vector.memset(new[:, :, F:XW], 0.0).then_inc(const_dve, 1)
            for c in range(C):
                fits = sum(P for cap in CAPS if cap >= DMAX - c)
                nc.vector.memset(limit[:, c:c + 1], float(fits)).then_inc(const_dve, 1)
            dve.wait_ge(const_dve, C + 1)
            dve.wait_ge(const_pool, 11)

            def search(t, b):
                dve.wait_ge(sq_done, t + 1)
                part = sq[b][:, POOL_BLK * BLK:N].rearrange("p (n w) -> p n w", w=BLK)
                nc.vector.tensor_tensor(part, part, pos[:, None, :].broadcast_to([P, NBLK - POOL_BLK, BLK]),
                                        ALU.mult).then_inc(key_dve, 1)
                dve.wait_ge(key_dve, t + 1)
                dve.wait_ge(key_pool, t + 1)
                dve.sem_inc(passed, 1)
                for n in range(NBLK):
                    last = nc.vector.max(cand[:, b, n, :], sq[b][:, n * BLK:(n + 1) * BLK])
                last.then_inc(max_done, 1)

            def lists(i):
                both = [(b, 2 * i + b) for b in range(2)]
                for b, t in both:
                    dve.wait_ge(max_done, t + 1)
                    nc.vector.tensor_tensor(cand_b[:, b], cand[:, b], blk_base[:], ALU.add).then_inc(cb_done, 1)
                for b, t in both:
                    dve.wait_ge(cb_done, t + 1)
                    nc.vector.scalar_tensor_tensor(
                        out=cand_g[:, b, :], in0=cand[:, b].rearrange("p n k -> p (n k)"), scalar=0.0,
                        in1=cand_b[:, b].rearrange("p n k -> p (n k)"), op0=ALU.is_gt, op1=ALU.mult).then_inc(cg_done, 1)
                for b, t in both:
                    dve.wait_ge(cg_done, t + 1)
                    nc.vector.scalar_tensor_tensor(out=cand_g[:, b, :], in0=cand_g[:, b, :], scalar=node_f[:, bass.ds(t, 1)],
                                                   in1=cand_g[:, b, :], op0=ALU.not_equal, op1=ALU.mult).then_inc(self_out, 1)
                at_least(dve, lst_free, 2 * i)
                ROUNDS = KMAX // TOP
                for r in range(ROUNDS):
                    for b, t in both:
                        if r:
                            dve.wait_ge(round_done[b], (2 * ROUNDS - 1) * i + 2 * r)
                        else:
                            dve.wait_ge(self_out, t + 1)
                        dve.sem_inc(passed, 1)
                        nc.vector.max(lst[:, b, r * TOP:(r + 1) * TOP], cand_g[:, b, :]).then_inc(round_done[b], 1)
                    for b, t in both:
                        if r < ROUNDS - 1:
                            dve.wait_ge(round_done[b], (2 * ROUNDS - 1) * i + 2 * r + 1)
                            dve.sem_inc(passed, 1)
                            nc.vector.match_replace(cand_g[:, b, :], lst[:, b, r * TOP:(r + 1) * TOP],
                                                    cand_g[:, b, :], 0.0).then_inc(round_done[b], 1)
                for b, t in both:
                    dve.wait_ge(round_done[b], (2 * ROUNDS - 1) * (i + 1))
                    nc.vector.tensor_scalar(lst_c[:, b, :], lst[:, b, :], 0.0, 0.0, ALU.is_gt, ALU.add,
                                            accum_out=deg[:, bass.ds(t, 1)]).then_inc(deg_done, 1)

            for first, last in ((0, 1), (1, PAIRS)):
                for i in pairs_of(dve, first, last):
                    for b in range(2):
                        t = 2 * i + b
                        dve.wait_ge(x_in[b], 16 * (i + 1))
                        node_dve_stats(dve, b, t, new[:, b, 0:F])
                        search(t, b)
                        node_dve_norm(dve, b, t, new[:, b, 0:F])
                    lists(i)

            steps = [0]

            def step(ins):
                steps[0] += 1
                ins.then_inc(dv, 1)
                dve.wait_ge(dv, steps[0])

            def by_class(t):
                return t.rearrange("p (c t) -> p c t", c=C)

            dve.wait_ge(deg_done, T)
            step(nc.vector.tensor_tensor(by_class(eq), deg[:, None, :].broadcast_to([P, C, T]),
                                         cls[:, :, None].broadcast_to([P, C, T]), ALU.is_equal))
            step(nc.vector.memset(ones_ct, 1.0))
            dve.wait_ge(tot_ps, 1)
            nc.vector.tensor_copy(totals, rank_ps[:, 0:CT]).then_inc(tot_sb, 1)
            dve.wait_ge(tot_sb, 1)
            step(nc.vector.tensor_tensor_scan(scan, ones_ct, totals, 0.0, ALU.mult, ALU.add))
            step(nc.vector.tensor_tensor(scan, scan, totals, ALU.subtract))
            dve.wait_ge(tri_ps, 1)
            step(nc.vector.tensor_tensor(value, rank_ps[:, 0:CT], scan, ALU.add))
            step(nc.vector.tensor_tensor(value, value, eq, ALU.mult))
            step(nc.vector.tensor_reduce(rank[:], by_class(value).rearrange("p c t -> p t c"), AX_X, ALU.add))
            step(nc.vector.tensor_copy(rank_u[:], rank[:]))
            step(nc.vector.tensor_tensor(by_class(totals), by_class(value),
                                         limit[:, :, None].broadcast_to([P, C, T]), ALU.is_ge))
            step(nc.vector.tensor_reduce(bad[:, 0:1], totals, AX_X, ALU.add))
            dve.wait_ge(sq_done, T)
            step(nc.vector.scalar_tensor_tensor(out=flags[:], in0=deg[:], scalar=1.0, in1=squares[:],
                                                op0=ALU.add, op1=ALU.not_equal))
            step(nc.vector.tensor_reduce(bad[:, 1:2], flags[:], AX_X, ALU.add))
            dve.wait_ge(plain_done, T)
            step(nc.vector.tensor_tensor(flags[:], plain[:], squares[:], ALU.not_equal))
            step(nc.vector.tensor_reduce(bad[:, 3:4], flags[:], AX_X, ALU.add))
            step(nc.vector.tensor_scalar(flags[:], deg[:], float(DMAX), None, ALU.is_gt))
            step(nc.vector.tensor_reduce(bad[:, 2:3], flags[:], AX_X, ALU.add))
            step(nc.vector.tensor_reduce(bad_sum[:], bad[:, 0:4], AX_X, ALU.add))
            nc.vector.sem_inc(bad_ps, 1)
            dve.wait_ge(bad_ps, 2)
            nc.vector.tensor_copy(verdict[:], hw_ps[0][:, 0:1]).then_inc(verdict_done, 1)
            dve.wait_ge(verdict_done, 1)
            v = dve.value_load(verdict[0:1, 0:1], min_val=0, max_val=2 ** 30)

            def layer_tile(x_):
                l, b, g, t, s = x_.l, x_.b, x_.g, x_.n, x_.s
                t = s - 2 * SP_PAIRS * l
                cap = x_.cap + 1
                G = gath[b][:, 0:cap, :]
                feats = G[:, :, 0:F]
                dve.wait_ge(row_in[b], 16 * (x_.used + 1))
                dve.wait_ge(g_in[b], 16 * x_.gathered)
                dve.wait_ge(own_done, s + 1)
                if l < 3:
                    nc.vector.tensor_scalar(e1[:, 0:cap], G[:, :, F], row[:, b, X_S:X_S + 1], None,
                                            ALU.add).then_inc(e1_done, 1)
                    dve.wait_ge(e1_done, s + 1)
                    nc.vector.scalar_tensor_tensor(out=e2[:, b, 0:cap], in0=e1[:, 0:cap], scalar=SLOPE,
                                                   in1=e1[:, 0:cap], op0=ALU.mult, op1=ALU.max).then_inc(e2_done, 1)
                    dve.wait_ge(e2_done, s + 1)
                    nc.vector.tensor_reduce(emax[:], e2[:, b, 0:cap], AX_X, ALU.max).then_inc(emax_done, 1)
                    dve.wait_ge(emax_done, s + 1)
                    nc.vector.tensor_scalar(nemax[:, b:b + 1], emax[:], -1.0, None, ALU.mult).then_inc(nemax_done, 1)
                    weights = prob[:, b, 0:cap]
                if l in (0, 2):
                    dve.wait_ge(prob_done, s + 1)
                    nc.vector.reciprocal(rsum[:], psum_p[:, b:b + 1]).then_inc(rsum_done, 1)
                    factor, ready = rsum, (rsum_done, s + 1)
                if l == 1:
                    nc.vector.tensor_scalar(ok[:, 0:cap], G[:, :, F], FAR / 10, 0.0, ALU.is_gt, ALU.add,
                                            accum_out=count[:]).then_inc(ok_done, 1)
                    dve.wait_ge(ok_done, t + 1)
                    dve.wait_ge(prob_done, s + 1)
                    nc.vector.scalar_tensor_tensor(out=pok[:, 0:cap], in0=prob[:, b, 0:cap], scalar=1.0,
                                                   in1=ok[:, 0:cap], op0=ALU.mult, op1=ALU.mult,
                                                   accum_out=sums[:]).then_inc(pok_done, 1)
                    dve.wait_ge(pok_done, t + 1)
                    nc.vector.tensor_scalar(top[:], sums[:], 1e-30, None, ALU.max).then_inc(sums_done, 1)
                    dve.wait_ge(sums_done, t + 1)
                    nc.vector.reciprocal(rsum[:], top[:]).then_inc(rsum_done, 1)
                    dve.wait_ge(rsum_done, s + 1)
                    nc.vector.tensor_scalar(share[:, 0:cap], pok[:, 0:cap], rsum[:], None, ALU.mult).then_inc(share_done, 1)
                    dve.wait_ge(share_done, t + 1)
                    nc.vector.tensor_reduce(top[:], share[:, 0:cap], AX_X, ALU.max).then_inc(top_done, 1)
                    nc.vector.scalar_tensor_tensor(out=wgt[:, 0:cap], in0=share[:, 0:cap], scalar=THR,
                                                   in1=share[:, 0:cap], op0=ALU.is_ge, op1=ALU.mult).then_inc(wgt_done, 1)
                    dve.wait_ge(top_done, t + 1)
                    nc.vector.tensor_scalar(fac[:], top[:], THR, count[:], ALU.is_gt, ALU.mult).then_inc(fac_done, 1)
                    dve.wait_ge(wgt_done, t + 1)
                    weights = wgt[:, 0:cap]
                    factor, ready = fac, (fac_done, t + 1)
                if l < 3:
                    nc.vector.tensor_tensor(feats, feats, weights[:, :, None].broadcast_to([P, cap, F]),
                                            ALU.mult).then_inc(gw_done, 1)
                    dve.wait_ge(gw_done, s + 1)
                else:
                    dve.wait_ge(x_new, g)
                nc.vector.tensor_reduce(agg[:], feats.rearrange("p k f -> p f k"), AX_X,
                                        ALU.add if l < 3 else ALU.max).then_inc(agg_done[b], 1)
                dve.wait_ge(agg_done[b], x_.used + 1)
                if l < 3:
                    dve.wait_ge(*ready)
                    finish_tile(x_, agg[:], factor)
                    return
                at_least(dve, res_out[b], 16 * x_.u)
                dve.wait_ge(kept_out[b], 16 * uses(3, b))
                nc.vector.tensor_tensor(new[:, b, 0:F], agg[:], row[:, b, 0:F], ALU.add).then_inc(x_new, 1)

            def finish_tile(x_, sums_, factor):
                l, b, g = x_.l, x_.b, x_.g
                x_row = row[:, b, 0:F]
                at_least(dve, kept_out[b], 16 * x_.used)
                if l == 2:
                    nc.vector.scalar_tensor_tensor(out=new[:, b, 0:F], in0=sums_, scalar=factor[:], in1=x_row,
                                                   op0=ALU.mult, op1=ALU.add).then_inc(x_new, 1)
                else:
                    elu_residual(dve, g, b, l, factor, x_row, sums_)
                dve.wait_ge(x_new, g + 1)
                node_dve_stats(dve, b, x_.m, new[:, b, 0:F])
                node_dve_norm(dve, b, x_.m, new[:, b, 0:F])
                if l == 0:
                    mark_unattendable(dve, b, x_.n)

            def least_t(l):
                dve.wait_ge(w_tT_sb, l + 1)
                nc.vector.scalar_tensor_tensor(out=w_live, in0=w_tT[:], scalar=FAR / 10, in1=w_tT[:],
                                               op0=ALU.is_gt, op1=ALU.mult).then_inc(w_live_done, 1)
                dve.wait_ge(w_live_done, l + 1)
                nc.vector.tensor_reduce(w_tile_min, w_live, AX_X, ALU.min).then_inc(w_min_done, 1)
                dve.wait_ge(w_min_done, l + 1)

            def wide_prep(l):
                dve.wait_ge(w_t_in, 32 * (l + 1))
                nc.vector.tensor_reduce(w_min[:], w_mins[:], AX_X, ALU.min).then_inc(w_prep, 1)
                dve.wait_ge(w_prep, 2 * l + 1)
                nc.vector.tensor_scalar(w_min1[:], w_min[:], 1.0, None, ALU.subtract).then_inc(w_prep, 1)
                dve.wait_ge(w_prep, 2 * l + 2)
                nc.vector.tensor_scalar(w_t, w_t, w_min1[:], 0.0, ALU.subtract, ALU.max).then_inc(w_ready, 1)

            def wide_cols(x_):
                dve.wait_ge(w_s_in, 16 * (x_.used + 1))
                at_least(dve, w_u_done, x_.used)
                dve.wait_ge(w_ready, x_.l + 1)
                nc.vector.tensor_tensor(w_us[:], w_s[:, 1:2], w_min1[:], ALU.add).then_inc(w_cols, 1)

            def wide_max(x_):
                dve.wait_ge(w_adj_in, 16 * (x_.used + 1))
                dve.sem_inc(passed, 1)
                nc.vector.tensor_tensor_reduce(out=w_adj, in0=w_adj.bitcast(I32), in1=w_t, scale=1.0, scalar=0.0,
                                               op0=ALU.mult, op1=ALU.max, accum_out=w_max[:]).then_inc(w_max_done, 1)
                dve.wait_ge(w_max_done, x_.used + 1)
                dve.wait_ge(w_cols, x_.used + 1)
                nc.vector.tensor_tensor(w_u[:], w_max[:], w_us[:], ALU.add).then_inc(w_steps, 1)
                dve.wait_ge(w_steps, 2 * x_.used + 1)
                nc.vector.scalar_tensor_tensor(out=w_m[:], in0=w_u[:], scalar=SLOPE, in1=w_u[:],
                                               op0=ALU.mult, op1=ALU.max).then_inc(w_steps, 1)
                dve.wait_ge(w_steps, 2 * x_.used + 2)
                nc.vector.tensor_scalar(w_negm[:], w_m[:], -1.0, None, ALU.mult).then_inc(w_m_done, 1)

            def wide_lrelu(x_):
                dve.wait_ge(w_u_done, x_.used + 1)
                nc.vector.scalar_tensor_tensor(out=w_e, in0=w_e, scalar=SLOPE, in1=w_e,
                                               op0=ALU.mult, op1=ALU.max).then_inc(w_lrelu_done, 1)

            def wide_weights(x_):
                dve.wait_ge(w_exp_done, x_.used + 1)
                nc.vector.scalar_tensor_tensor(out=w_e, in0=w_adj, scalar=0.0, in1=w_e, op0=ALU.is_gt,
                                               op1=ALU.mult, accum_out=w_sum[:]).then_inc(w_p_done, 1)
                dve.wait_ge(w_p_done, x_.used + 1)
                if x_.l != 1:
                    nc.vector.reciprocal(w_rs[:], w_sum[:]).then_inc(w_rs_done, 1)
                    dve.wait_ge(w_rs_done, x_.used + 1)

            def wide_threshold(x_):
                k1 = x_.used - ND
                nc.vector.tensor_scalar(w_u[:], w_sum[:], 1e-30, None, ALU.max).then_inc(w_s1_done, 1)
                dve.wait_ge(w_s1_done, k1 + 1)
                nc.vector.tensor_scalar(w_s1[:], w_u[:], THR, None, ALU.mult).then_inc(w_s2_done, 1)
                nc.vector.reciprocal(w_rs[:], w_u[:]).then_inc(w_rs_done, 1)
                dve.wait_ge(w_s2_done, k1 + 1)
                nc.vector.scalar_tensor_tensor(out=w_e, in0=w_e, scalar=w_s1[:], in1=w_e,
                                               op0=ALU.is_ge, op1=ALU.mult).then_inc(w_thr_done, 1)
                dve.wait_ge(w_rs_done, x_.used + 1)
                dve.wait_ge(w_cnt_done, k1 + 1)
                nc.vector.tensor_scalar(w_m[:], w_rs[:], THR, w_cnt[:], ALU.is_gt, ALU.mult).then_inc(w_s3_done, 1)
                dve.wait_ge(w_s3_done, k1 + 1)
                nc.vector.tensor_tensor(w_fac[:], w_rs[:], w_m[:], ALU.mult).then_inc(w_fac_done, 1)
                dve.wait_ge(w_fac_done, k1 + 1)
                dve.wait_ge(w_thr_done, k1 + 1)

            def wide_finish(x_):
                dve.wait_ge(row_in[WIDE], 16 * (x_.used + 1))
                dve.wait_ge(w_multiplied, NQ * (x_.used + 1))
                finish_tile(x_, acc_ps, w_fac if x_.l == 1 else w_rs)

            with dve.If(v < 1):
                for l in range(3):
                    least_t(l)
                    for first, last, caps in turns:
                        for k in pairs_of(dve, first, last):
                            wide = wide_tile(l, k)
                            for j in range(len(caps)):
                                layer_tile(gathered_tile(l, k, first, caps, j))
                                if j == 0 and first and last < TURNS:
                                    wide_cols(wide)
                                if j == 1 and first:
                                    wide_finish(wide_tile(l, k - 1))
                                if last == TURNS:
                                    continue
                                if j == 1:
                                    if first == 0:
                                        wide_prep(l)
                                        wide_cols(wide)
                                    wide_max(wide)
                                if j == 2:
                                    wide_lrelu(wide)
                                if j == 3:
                                    wide_weights(wide)
                                if j == 4 and l == 1:
                                    wide_threshold(wide)
                for first, last, cap in groups:
                    for i in pairs_of(dve, first, last):
                        for b in range(2):
                            layer_tile(last_layer_tile(i, first, cap, b))
            with dve.Else():
                dense_dve(dve)


def kernel(x, adj, L0_gnn_W, L0_gnn_a, L1_gnn_W, L1_gnn_a, L2_gnn_attn):
    import numpy as np
    import concourse.bacc as bacc
    from concourse.bass_utils import run_bass_kernel_spmd

    given = {"x": x, "adj": adj, "w0": L0_gnn_W, "a0": L0_gnn_a, "w1": L1_gnn_W, "a1": L1_gnn_a, "a2": L2_gnn_attn}
    arrays = {name: np.ascontiguousarray(a) for name, a in given.items()}
    nc = bacc.Bacc("TRN2", target_bir_lowering=False, num_devices=1)
    args = [nc.dram_tensor(n, a.shape, mybir.dt.from_np(a.dtype), kind="ExternalInput").ap() for n, a in arrays.items()]
    out = nc.dram_tensor("out", x.shape, F32, kind="ExternalOutput").ap()
    build(nc, *args, out)
    r = run_bass_kernel_spmd(nc, [arrays], core_ids=[0])
    return r.results[0]["out"]
```
